# Optimizing a Trainium2 kernel written in Bass

```python
import numpy as np
import jax
import jax.numpy as jnp

def _softmax(x, axis=-1):
    return jax.nn.softmax(x, axis=axis)

def _gelu(x):
    return jax.nn.gelu(x, approximate=True)

def _silu(x):
    return jax.nn.silu(x)

def _sigmoid(x):
    return jax.nn.sigmoid(x)

def _layernorm(x, axis=-1, eps=1e-05):
    m = jnp.mean(x, axis=axis, keepdims=True)
    v = jnp.var(x, axis=axis, keepdims=True)
    return (x - m) / jnp.sqrt(v + eps)

def _scatter_add(tgt, idx, src, axis=0):
    return tgt.at[idx].add(src)

def _segment_sum(src, seg, n):
    return jax.ops.segment_sum(src, seg, n)
kernel_name = 'mk_lm_tower_d1_tok_ids1024_r4_1207b3'

def setup_inputs(seed: int=0):
    np.random.seed(seed)
    _w = jnp.asarray

    def _rec_inputs():
        import jax
        import jax.numpy as jnp
        _rk = jax.random.key(seed)
        x = jax.random.randint(jax.random.fold_in(_rk, 1), (2, 2048), 0, 50257, jnp.int32)
        return x
    x = _rec_inputs()

    def _L0_tok_setup():
        import jax, jax.numpy as jnp
        import numpy as np
        VOCAB, RANK, EMB = (50257, 64, 256)
        key = jax.random.key(seed)
        k1, k2, k3 = jax.random.split(key, 3)
        x = jax.random.randint(k1, (8, 1024), 0, VOCAB)
        A = jax.random.normal(k2, (VOCAB, RANK), dtype=jnp.float32) * 0.02
        B = jax.random.normal(k3, (RANK, EMB), dtype=jnp.float32) * 0.02
        return {'x': x, 'A': A, 'B': B}
    _L0_tok_all = _L0_tok_setup()
    _L0_tok_in = {k: v for k, v in _L0_tok_all.items() if k in ('A', 'B')}
    del _L0_tok_all

    def _L0_attn_setup():
        import jax, jax.numpy as jnp
        import numpy as np
        import math
        N, S, E, H = (4, 1024, 256, 16)
        D = E // H
        key = jax.random.key(seed)
        ks = jax.random.split(key, 9)
        w = 1.0 / math.sqrt(E)
        mk = lambda k, shape: jax.random.normal(k, shape, jnp.float32) * w
        return {'x': jax.random.normal(ks[0], (N, S, E), jnp.float32), 'Wq': mk(ks[1], (E, E)), 'bq': mk(ks[2], (E,)), 'Wk': mk(ks[3], (E, E)), 'bk': mk(ks[4], (E,)), 'Wv': mk(ks[5], (E, E)), 'bv': mk(ks[6], (E,)), 'Wo': mk(ks[7], (E, E)), 'bo': mk(ks[8], (E,))}
    _L0_attn_all = _L0_attn_setup()
    _L0_attn_in = {k: v for k, v in _L0_attn_all.items() if k in ('Wq', 'bq', 'Wk', 'bk', 'Wv', 'bv', 'Wo', 'bo')}
    del _L0_attn_all

    def _L0_ffn_setup():
        import jax, jax.numpy as jnp
        import numpy as np
        CAP_FACTOR = 1.5
        key = jax.random.key(seed)
        ks = jax.random.split(key, 6)
        E, S, D, M = (48, 4, 256, 256)
        K = D // S
        x = jax.random.normal(ks[0], (4, 1024, D), dtype=jnp.float32)
        Wr = jax.random.normal(ks[1], (E, D), dtype=jnp.float32) * 0.02
        W1 = jax.random.normal(ks[2], (E, S, D, M), dtype=jnp.float32) * (1.0 / np.sqrt(D))
        b1 = jnp.zeros((E, S, M), dtype=jnp.float32)
        W2 = jax.random.normal(ks[3], (E, S, M, K), dtype=jnp.float32) * (1.0 / np.sqrt(M))
        b2 = jnp.zeros((E, S, K), dtype=jnp.float32)
        return {'x': x, 'Wr': Wr, 'W1': W1, 'b1': b1, 'W2': W2, 'b2': b2}
    _L0_ffn_all = _L0_ffn_setup()
    _L0_ffn_in = {k: v for k, v in _L0_ffn_all.items() if k in ('Wr', 'W1', 'b1', 'W2', 'b2')}
    del _L0_ffn_all
    return {'x': x, 'L0_tok_A': _L0_tok_in['A'], 'L0_tok_B': _L0_tok_in['B'], 'L0_attn_Wq': _L0_attn_in['Wq'], 'L0_attn_bq': _L0_attn_in['bq'], 'L0_attn_Wk': _L0_attn_in['Wk'], 'L0_attn_bk': _L0_attn_in['bk'], 'L0_attn_Wv': _L0_attn_in['Wv'], 'L0_attn_bv': _L0_attn_in['bv'], 'L0_attn_Wo': _L0_attn_in['Wo'], 'L0_attn_bo': _L0_attn_in['bo'], 'L0_ffn_Wr': _L0_ffn_in['Wr'], 'L0_ffn_W1': _L0_ffn_in['W1'], 'L0_ffn_b1': _L0_ffn_in['b1'], 'L0_ffn_W2': _L0_ffn_in['W2'], 'L0_ffn_b2': _L0_ffn_in['b2']}

def reference(x, L0_tok_A, L0_tok_B, L0_attn_Wq, L0_attn_bq, L0_attn_Wk, L0_attn_bk, L0_attn_Wv, L0_attn_bv, L0_attn_Wo, L0_attn_bo, L0_ffn_Wr, L0_ffn_W1, L0_ffn_b1, L0_ffn_W2, L0_ffn_b2):
    import jax
    import jax.numpy as jnp

    def _L0_tok_ref(x, A, B):
        import jax, jax.numpy as jnp
        import numpy as np
        VOCAB, RANK, EMB = (50257, 64, 256)
        return jnp.einsum('bsr,re->bse', A[x], B)

    def _L0_attn_ref(x, Wq, bq, Wk, bk, Wv, bv, Wo, bo):
        import jax, jax.numpy as jnp
        import numpy as np
        import math
        N, S, E, H = (4, 1024, 256, 16)
        D = E // H
        n, s, e = x.shape
        h, d = (H, D)
        scale = 1.0 / math.sqrt(d)

        def proj(W, b):
            y = jnp.einsum('nse,fe->nsf', x, W) + b
            return y.reshape(n, s, h, d).transpose(0, 2, 1, 3)
        Q = proj(Wq, bq)
        K = proj(Wk, bk)
        V = proj(Wv, bv)
        scores = jnp.einsum('nqhd,nkhd->nhqk', Q, K) * scale
        attn = jax.nn.softmax(scores, axis=-1)
        out = jnp.einsum('nhql,nlhd->nqhd', attn, V)
        out = out.reshape(n, s, e)
        return jnp.einsum('nse,fe->nsf', out, Wo) + bo

    def _L0_ffn_ref(x, Wr, W1, b1, W2, b2):
        import jax, jax.numpy as jnp
        import numpy as np
        CAP_FACTOR = 1.5
        orig_shape = x.shape
        D = x.shape[-1]
        E = Wr.shape[0]
        xf = x.reshape(-1, D)
        T = xf.shape[0]
        cap = int(CAP_FACTOR * T / E)
        logits = xf @ Wr.T
        vals, idx = jax.lax.top_k(logits.T, cap)
        w = jax.nn.softmax(vals, axis=-1)
        xg = xf[idx]
        h = jax.nn.gelu(jnp.einsum('ecd,esdm->ecsm', xg, W1) + b1[:, None], approximate=False)
        y = jnp.einsum('ecsm,esmk->ecsk', h, W2) + b2[:, None]
        y = y.reshape(E, cap, D) * w[..., None]
        out = jnp.zeros_like(xf).at[idx.reshape(-1)].add(y.reshape(-1, D))
        return out.reshape(orig_shape)
    h = _L0_tok_ref(x, L0_tok_A, L0_tok_B)
    h = h + _L0_attn_ref(_layernorm(h, axis=-1), L0_attn_Wq, L0_attn_bq, L0_attn_Wk, L0_attn_bk, L0_attn_Wv, L0_attn_bv, L0_attn_Wo, L0_attn_bo)
    h = h + _L0_ffn_ref(_layernorm(h, axis=-1), L0_ffn_Wr, L0_ffn_W1, L0_ffn_b1, L0_ffn_W2, L0_ffn_b2)
    return h

_drawn_inputs = setup_inputs


def setup_inputs(seed=0):
    import zlib

    import numpy as np

    out = dict(_drawn_inputs(seed))
    spreads = {'L0_ffn_b1': (0.0, 2.0), 'L0_ffn_b2': (0.0, 0.8)}
    factors = {}
    for name, (base, spread) in spreads.items():
        noise = np.random.default_rng([zlib.crc32(name.encode()), seed]).standard_normal(out[name].shape)
        drawn = base * np.exp(spread * noise) if base else spread * noise
        out[name] = jnp.asarray(drawn.astype(out[name].dtype))
    for name, factor in factors.items():
        out[name] = (out[name] * factor).astype(out[name].dtype)
    return out
```

```python
from contextlib import ExitStack

import concourse.bass as bass
from concourse import mybir

P = 128
F32 = mybir.dt.float32
BF16 = mybir.dt.bfloat16
I32 = mybir.dt.int32
U32 = mybir.dt.uint32
ALU = mybir.AluOpType
ACT = mybir.ActivationFunctionType
AX = mybir.AxisListType
LN_EPS = 1e-5
LOWEST = -3.0e38


def wait_from_first(eng, sem, count):
    if isinstance(count, int) and count <= 0:
        return
    eng.wait_ge(sem, count)


def tower_kernel(nc, ids, A, B, WqT, WkT, WvT, WoT, bqkv, bo, WrT, W1, b1T, W2, b2, out):
    RANK, E = B.shape
    NX, _, EW = W1.shape
    T = ids.shape[0] * ids.shape[1]
    NB, S = 2, T // 2
    NT = T // P
    H, D = 16, E // 16
    NH2 = E // P
    CH = 512
    TC = CH // P
    NC = T // CH
    QT = S // P
    SUB = 4
    MID = EW // (NH2 * SUB)
    MH = MID // P
    KO = E // SUB
    CAP = int(1.5 * T / NX)
    SCALE = 1.0 / float(D) ** 0.5
    G = CH // 8
    assert CAP == P and NB * NX <= P and NC % 2 == 0 and G == 64 and 8 * D == P and H == D

    h_dram = nc.dram_tensor("h_dram", [T, E], F32).ap()
    qkv_dram = nc.dram_tensor("qkv_dram", [NC, 3, E, CH], F32).ap()
    xn_dram = nc.dram_tensor("xn_dram", [T, E], F32).ap()

    ctx = ExitStack()
    with ctx:
        def sb(name, shape, dt=F32):
            return ctx.enter_context(nc.sbuf_tensor(name, shape, dt))

        def sem(name):
            return ctx.enter_context(nc.semaphore(name))

        big = sb("big", [P, 4 * P * G])
        q_bd = [big[:, n * P * G:(n + 1) * P * G].rearrange("p (m g) -> p m g", g=G) for n in (0, 1)]
        v_bd = [big[:, n * P * G:(n + 1) * P * G].rearrange("p (m g) -> p m g", g=G) for n in (2, 3)]
        WN = EW + SUB * MH * KO
        WB = 4
        WS = 12
        w_slot = [big[:, s * WN:(s + 1) * WN] for s in range(WS)]
        k_op = sb("k_op", [P, 2, H, G])
        y_t = sb("y_t", [P, NH2, NB, H, P])
        work = sb("work", [P, 5760])
        ident = sb("ident", [P, P])
        eps = sb("eps", [P, 1])
        pad = sb("pad", [P, 2])
        ids_sb = sb("ids_sb", [P, NT], I32)
        b_sb = sb("b_sb", [2 * RANK, E])
        bqkv_sb = sb("bqkv_sb", [P, 3 * NH2])
        bo_sb = sb("bo_sb", [P, E])
        wo_sb = sb("wo_sb", [P, NH2, E])
        wr_sb = sb("wr_sb", [P, NH2, NX])
        b1_sb = sb("b1_sb", [P, NX * SUB * MH])
        bn6 = sb("bn6", [P, 2, 6])
        mean_var = sb("mean_var", [P, 2, 2])
        std = sb("std", [P, 2])
        rstd = sb("rstd", [P, 2])
        rows_sb = sb("rows_sb", [P, 2 * TC, RANK])

        def carve(base, at, n):
            return base[:, at:at + n], at + n

        at = 0
        wqkv_sb, at = carve(work, at, 3 * NH2 * E)
        wqkv_sb = wqkv_sb.rearrange("p (w h e) -> p w h e", w=3, h=NH2)
        xnT, at = carve(work, at, 2 * NH2 * CH)
        xnT = xnT.rearrange("p (k h t) -> p k h t", k=2, h=NH2)
        rowsT, at = carve(work, at, P)
        h_sb, at = carve(work, at, 2 * E)
        h_sb = h_sb.rearrange("p (k e) -> p k e", k=2)
        xn, at = carve(work, at, 2 * E)
        xn = xn.rearrange("p (k e) -> p k e", k=2)
        prob = sb("prob", [P, G, H])
        prob_t = sb("prob_t", [P, G * H])
        row_max = sb("row_max", [P, G])
        row_sum = sb("row_sum", [P, G])
        qkv_sb, at = carve(work, at, 2 * CH)
        qkv_sb = qkv_sb.rearrange("p (k t) -> p k t", k=2)
        assert at <= 5760
        at = 0
        res_sb, at = carve(work, at, 2 * E)
        res_sb = res_sb.rearrange("p (k e) -> p k e", k=2)
        h2_sb, at = carve(work, at, 2 * E)
        h2_sb = h2_sb.rearrange("p (k e) -> p k e", k=2)
        xn2, at = carve(work, at, 2 * E)
        xn2 = xn2.rearrange("p (k e) -> p k e", k=2)
        att_sb, at = carve(work, at, 2 * E)
        att_sb = att_sb.rearrange("p (k h r) -> p k h r", k=2, h=NH2)
        xn2T, at = carve(work, at, 2 * E)
        xn2T = xn2T.rearrange("p (k e) -> p k e", k=2)
        logits, at = carve(work, at, S)
        LP = 64 + NX
        assert at <= 5760
        y_flat = y_t[:, :, :, :, :].rearrange("p w b h r -> p (w b h r)")
        at = 0
        top, at = carve(y_flat, at, CAP)
        top_at, at = carve(y_flat, at, CAP)
        top_atf, at = carve(y_flat, at, CAP)
        topT, at = carve(y_flat, at, P)
        topiT, at = carve(y_flat, at, P)
        b2_sb, at = carve(y_flat, at, WB * E)
        b2_sb = b2_sb.rearrange("p (k e) -> p k e", k=WB)
        flip, at = carve(y_flat, at, P)
        first_row, at = carve(y_flat, at, P)
        ones, at = carve(y_flat, at, P)
        sel_mask, at = carve(y_flat, at, NX)
        sel_v, at = carve(y_flat, at, NX)
        sel_max, at = carve(y_flat, at, NX)
        sel_w, at = carve(y_flat, at, NX)
        sel_if, at = carve(y_flat, at, NX)
        sel_rden, at = carve(y_flat, at, NX)
        rev_if, at = carve(y_flat, at, NX)
        tok_idx, at = carve(y_flat, at, NX)
        tok_idx = tok_idx.bitcast(I32)
        at = 0
        xg, at = carve(work, at, 4 * E)
        xg = xg.rearrange("p (k e) -> p k e", k=4)
        xgT, at = carve(work, at, 2 * E)
        xgT = xgT.rearrange("p (k e) -> p k e", k=2)
        act, at = carve(work, at, 2 * SUB * MH * P)
        act = act.rearrange("p (k s t) -> p k s t", k=2, t=P)
        y_sb, at = carve(work, at, 4 * E)
        y_sb = y_sb.rearrange("p (k e) -> p k e", k=4)
        assert at <= 5760

        bank = [ctx.enter_context(nc.psum_tensor(f"bank{i}", [P, CH], F32)) for i in range(4)]
        sc_ps = ctx.enter_context(nc.psum_tensor("sc_ps", [P, 2, CH], F32))
        pt_ps = ctx.enter_context(nc.psum_tensor("pt_ps", [P, 2, CH], F32))

        s_const = sem("s_const")
        s_id = sem("s_id")
        s_zero = sem("s_zero")
        s_ids = sem("s_ids")
        s_w = sem("s_w")
        s_rows = [sem(f"s_rows{k}") for k in range(8)]
        s_rowsT = sem("s_rowsT")
        s_rowsT_sb = sem("s_rowsT_sb")
        s_h = sem("s_h")
        s_h_sb = sem("s_h_sb")
        s_h_st = [sem(f"s_h_st{k}") for k in range(2)]
        s_bn = sem("s_bn")
        s_mv = sem("s_mv")
        s_std = sem("s_std")
        s_rstd = sem("s_rstd")
        s_xn = sem("s_xn")
        s_xT = sem("s_xT")
        s_xT_sb = sem("s_xT_sb")
        s_qkv = sem("s_qkv")
        s_qkv_sb = sem("s_qkv_sb")
        s_qkv_st = [sem(f"s_qkv_st{k}") for k in range(2)]
        s_ops = [sem(f"s_ops{k}") for k in range(2)]
        s_sc = sem("s_sc")
        s_max = sem("s_max")
        s_sub = sem("s_sub")
        s_exp = sem("s_exp")
        s_sum = sem("s_sum")
        s_rsum = sem("s_rsum")
        s_prob = sem("s_prob")
        s_pt = sem("s_pt")
        s_pt_sb = sem("s_pt_sb")
        s_pv = sem("s_pv")
        s_y = sem("s_y")
        t_att = sem("t_att")
        t_res = [sem(f"t_res{k}") for k in range(2)]
        t_o = sem("t_o")
        t_add = sem("t_add")
        t_h2 = sem("t_h2")
        t_h2_st = [sem(f"t_h2_st{k}") for k in range(2)]
        t_bn = sem("t_bn")
        t_mv = sem("t_mv")
        t_std = sem("t_std")
        t_rstd = sem("t_rstd")
        t_xn = sem("t_xn")
        t_xn_st = [sem(f"t_xn_st{k}") for k in range(2)]
        t_xT = sem("t_xT")
        t_xT_sb = sem("t_xT_sb")
        t_lg = sem("t_lg")
        t_lg_sb = sem("t_lg_sb")
        c_fill = sem("c_fill")
        c_top = sem("c_top")
        c_T = sem("c_T")
        c_T_sb = sem("c_T_sb")
        c_rev = sem("c_rev")
        c_dve = sem("c_dve")
        c_exp = sem("c_exp")
        c_sum = sem("c_sum")
        c_done = sem("c_done")
        e_w = [sem(f"e_w{k}") for k in range(WS)]
        e_b2 = [sem(f"e_b2{k}") for k in range(WB)]
        e_xg = [sem(f"e_xg{k}") for k in range(4)]
        e_xgT = sem("e_xgT")
        e_xgT_sb = sem("e_xgT_sb")
        e_h = sem("e_h")
        e_act = sem("e_act")
        e_y = sem("e_y")
        e_yb = sem("e_yb")
        e_y_sb = sem("e_y_sb")
        e_out = sem("e_out")

        block = ctx.enter_context(nc.Block())

        PROJ = ((0,), (1, 2), (3, 4), (5,))
        OPS = 16 * 24
        prob_f = prob[:, :, :].rearrange("p g h -> p (g h)")

        def load_weights(eng, e, s):
            eng.dma_start(w_slot[s][:, 0:EW], W1[bass.ds(e, 1), :, :].rearrange("a p n -> (a p) n")).then_inc(e_w[s], 16)
            eng.dma_start(w_slot[s][:, EW:WN], W2[bass.ds(e, 1), :, :].rearrange("a p n -> (a p) n")).then_inc(e_w[s], 16)

        def embed_chunks(eng, step):
            for c in range(4):
                step(c, c % 2, True, c >= 1, c >= 2)
            with eng.Fori(2, NC // 2) as i:
                for u in range(2):
                    step(2 * i + u, u, True, True, True)
            step(NC, 0, False, True, True)
            step(NC + 1, 1, False, False, True)

        @block.sync
        def _(sp):
            sp.dma_start(ids_sb[:, :], ids).then_inc(s_ids, 16)
            for k in range(2):
                sp.dma_start(b_sb[k * RANK:(k + 1) * RANK, :], B).then_inc(s_w, 16)
            for n, w in enumerate((WqT, WkT, WvT)):
                sp.dma_start(wqkv_sb[:, n, :, :], w.rearrange("(h p) e -> p h e", p=P)).then_inc(s_w, 16)
            sp.dma_start(bqkv_sb[:, :], bqkv).then_inc(s_w, 16)
            sp.dma_start(wo_sb[:, :, :], WoT.rearrange("(h p) e -> p h e", p=P)).then_inc(s_w, 16)
            sp.dma_start(wr_sb[:, :, :], WrT.rearrange("(h p) e -> p h e", p=P)).then_inc(s_w, 16)
            sp.dma_start(bo_sb[:, :], bo.to_broadcast([P, E])).then_inc(s_w, 16)
            sp.dma_start(b1_sb[:, :], b1T).then_inc(s_w, 16)

            h_rows = h_dram.rearrange("(c b t u) e -> c t b u e", b=8, t=8, u=8)

            def store_h(c, j):
                k = j % 2
                sp.wait_ge(s_h_sb, c * TC + j + 1)
                for tt in range(2):
                    if j == TC - 1 and tt == 1:
                        wait_from_first(sp, s_pv, c - 2)
                    sp.dma_start(h_rows[bass.ds(c, 1), 2 * j + tt, :, :, :].rearrange("c b u e -> (c b) u e"),
                                 h_sb[G * tt:G * tt + G, k, :]).then_inc(s_h_st[k], 16)

            def store_qkv(c, n):
                sp.wait_ge(s_qkv_sb, 6 * c + n + 1)
                sp.dma_start(qkv_dram[bass.ds(c, 1), n // 2, (n % 2) * P:(n % 2) * P + P, :]
                             .rearrange("c f t -> (c f) t"), qkv_sb[:, n % 2, :]).then_inc(s_qkv_st[n % 2], 16)

            def load_operands(c, cp):
                sp.wait_ge(s_qkv_st[0], 48 * (c + 1))
                sp.wait_ge(s_qkv_st[1], 48 * (c + 1))
                for t in range(8):
                    r = slice(D * t, D * t + D)
                    src = [qkv_dram[bass.ds(c, 1), w, :, G * t:G * t + G] for w in range(3)]
                    sp.dma_start(q_bd[cp][r, H * t:H * t + H, :], src[0].rearrange("c (h d) g -> (c d) h g", d=D)
                                 ).then_inc(s_ops[cp], 16)
                    sp.dma_start(k_op[r, cp, :, :], src[1].rearrange("c (h d) g -> (c d) h g", d=D)
                                 ).then_inc(s_ops[cp], 16)
                    sp.dma_start(v_bd[cp][r, D * t:D * t + D, :], src[2].rearrange("c (h d) g -> (c h) d g", d=D)
                                 ).then_inc(s_ops[cp], 16)

            def sp_step(c, cp, front, project, attend):
                for j in range(TC):
                    if front:
                        store_h(c, j)
                    if project:
                        for n in PROJ[j]:
                            store_qkv(c - 1, n)
                if project:
                    if isinstance(c, int) and c == 1:
                        sp.wait_ge(s_zero, 4)
                    if not front:
                        sp.wait_ge(s_pv, c - 2)
                    load_operands(c - 1, 1 - cp)

            embed_chunks(sp, sp_step)

            sp.wait_ge(s_pv, NC)
            for s in range(WS):
                sp.dma_start(w_slot[s][:, 0:EW], W1[s, :, :]).then_inc(e_w[s], 16)
                sp.dma_start(w_slot[s][:, EW:WN], W2[s, :, :]).then_inc(e_w[s], 16)

            for k in range(2):
                sp.wait_ge(s_h_st[k], 2 * 16 * NT // 2)

            def load_res(t, k):
                wait_from_first(sp, t_add, t - 1)
                sp.dma_start(res_sb[:, k, :], h_dram[bass.ds(t * P, P), :]).then_inc(t_res[k], 16)

            def store_tile(t, k):
                sp.wait_ge(t_h2, t + 1)
                sp.dma_start(out[bass.ds(t * P, P), :], h2_sb[:, k, :]).then_inc(t_h2_st[k], 16)
                sp.wait_ge(t_xn, t + 1)
                sp.dma_start(xn_dram[bass.ds(t * P, P), :], xn2[:, k, :]).then_inc(t_xn_st[k], 16)

            load_res(0, 0)
            load_res(1, 1)
            with sp.Fori(0, NT // 2 - 1) as i:
                for k in range(2):
                    store_tile(2 * i + k, k)
                    load_res(2 * i + k + 2, k)
            for k in range(2):
                store_tile(NT - 2 + k, k)

            sp.wait_ge(t_att, NT)
            for e in range(WB):
                sp.dma_start(b2_sb[:, e, :], b2[e:e + 1, :].to_broadcast([P, E])).then_inc(e_b2[e], 16)

            def refill(e, s):
                new = sp.snap(e + WS)
                """Expert e + WS's weights and expert e + WB's bias, in the place of expert e's."""
                sp.wait_ge(e_y, e + 1)
                load_weights(sp, new, s)
                refill_bias(e, s)

            def refill_bias(e, s):
                sp.wait_ge(e_yb, e + 1)
                sp.dma_start(b2_sb[:, s % WB, :], b2[bass.ds(e + WB, 1), :].to_broadcast([P, E])
                             ).then_inc(e_b2[s % WB], 16)

            with sp.Fori(0, NX // WS - 1) as i:
                for s in range(WS):
                    refill(i * WS + s, s)
            for s in range(WS - WB):
                refill_bias(NX - WS + s, s)
            sp.wait_ge(e_out, 16 * NX)

        @block.gpsimd
        def _(pool):
            pool.memset(ident[:, :], 0.0).then_inc(s_id, 1)
            pool.memset(eps[:, :], LN_EPS).then_inc(s_const, 1)
            pool.wait_ge(s_id, 1)
            pool.affine_select(out=ident[:, :], in_=ident[:, :], compare_op=ALU.not_equal, fill=1.0,
                               base=0, pattern=[[-1, P]], channel_multiplier=1).then_inc(s_const, 1)
            for n in range(2):
                pool.memset(v_bd[n][:, :, :], 0.0).then_inc(s_zero, 1)

            pool.wait_ge(s_ids, 16)
            for t in range(NT):
                k = t % (2 * TC)
                if t >= 2 * TC:
                    pool.wait_ge(s_rowsT, (t - 2 * TC) // 2 + 1)
                pool.indirect_dma_start(out=rows_sb[:, k, :], out_offset=None, in_=A,
                                        in_offset=bass.IndirectOffsetOnAxis(ap=ids_sb[:, t:t + 1], axis=0)
                                        ).then_inc(s_rows[k], 16)

            pool.wait_ge(s_y, 2 * NC)

            def lay_tile(t, b, tt, k):
                wait_from_first(pool, t_o, t - 1)
                pool.tensor_copy(att_sb[:, k, :, :],
                                 y_t[:, :, bass.ds(b, 1), bass.ds(tt, 1), :].rearrange("p h b t r -> p h (b t r)")
                                 ).then_inc(t_att, 1)

            lay_tile(0, 0, 0, 0)
            lay_tile(1, 0, 1, 1)
            with pool.Fori(1, NT // 2) as i:
                for k in range(2):
                    t = 2 * i + k
                    lay_tile(t, t // QT, t % QT, k)

            pool.wait_ge(t_att, NT)
            pool.memset(flip[:, :], 0.0).then_inc(s_id, 1)
            pool.memset(first_row[:, :], 0.0).then_inc(s_id, 1)
            pool.memset(ones[:, :], 1.0).then_inc(s_const, 1)
            pool.wait_ge(s_id, 3)
            pool.affine_select(out=flip[:, :], in_=flip[:, :], compare_op=ALU.not_equal, fill=1.0,
                               base=1 - P, pattern=[[1, P]], channel_multiplier=1).then_inc(s_const, 1)
            pool.affine_select(out=first_row[:, :], in_=first_row[:, :], compare_op=ALU.not_equal, fill=1.0,
                               base=0, pattern=[[0, P]], channel_multiplier=1).then_inc(s_const, 1)

            pool.wait_ge(c_done, 2)
            for k in range(2):
                pool.wait_ge(t_xn_st[k], 16 * NT // 2)
                pool.wait_ge(t_h2_st[k], 16 * NT // 2)

            def fetch(e):
                if e >= 4:
                    pool.wait_ge(e_xgT, e - 3)
                pool.indirect_dma_start(out=xg[:, e % 4, :], out_offset=None, in_=xn_dram,
                                        in_offset=bass.IndirectOffsetOnAxis(ap=tok_idx[:, e:e + 1], axis=0)
                                        ).then_inc(e_xg[e % 4], 16)

            def add_out(e):
                pool.wait_ge(e_y_sb, e + 1)
                if e > 0:
                    pool.wait_ge(e_out, 16 * e)
                pool.indirect_dma_start(out=out, out_offset=bass.IndirectOffsetOnAxis(ap=tok_idx[:, e:e + 1], axis=0),
                                        in_=y_sb[:, e % 4, :], in_offset=None, compute_op=ALU.add).then_inc(e_out, 16)

            for e in range(NX + 2):
                if e < NX:
                    fetch(e)
                if e >= 2:
                    add_out(e - 2)

        @block.tensor
        def _(pe):
            pe.wait_ge(s_const, 2)
            pe.wait_ge(s_w, 16 * 10)

            def embed(t, j, slot, use):
                k = j % 2
                if k == 0:
                    pe.wait_ge(s_rows[slot], 16 * use)
                    pe.wait_ge(s_rows[slot + 1], 16 * use)
                    wait_from_first(pe, s_xT_sb, t - 1)
                    pe.transpose(bank[0][:, 0:P], rows_sb[:, slot:slot + 2, :].rearrange("p k r -> p (k r)"),
                                 ident[:, :]).then_inc(s_rowsT, 1)
                    pe.wait_ge(s_rowsT_sb, t // 2 + 1)
                else:
                    wait_from_first(pe, s_xT_sb, t - 1)
                r = slice(RANK * k, RANK * k + RANK)
                pe.matmul(bank[k][:, 0:E], rowsT[r, :], b_sb[r, :], start=True, stop=True).then_inc(s_h, 1)

            def xn_transpose(t, k):
                pe.wait_ge(s_xn, t + 1)
                for h in range(NH2):
                    last = pe.transpose(bank[k][:, h * P:(h + 1) * P], xn[:, k, h * P:(h + 1) * P], ident[:, :])
                last.then_inc(s_xT, 1)

            def project(c, cp, n):
                if n == 0:
                    pe.wait_ge(s_xT_sb, (c + 1) * TC)
                wait_from_first(pe, s_qkv_sb, 6 * c + n - 1)
                f = (n % 2) * P
                for h in range(NH2):
                    last = pe.matmul(bank[2 + n % 2][:, :], wqkv_sb[:, n // 2, h, f:f + P], xnT[:, cp, h, :],
                                     start=(h == 0), stop=(h == NH2 - 1))
                last.then_inc(s_qkv, 1)

            def scores(c, cp):
                pe.wait_ge(s_ops[cp], OPS * ((c - cp) // 2 + 1))
                wait_from_first(pe, s_y, 2 * c)
                for g in range(G):
                    last = pe.matmul(sc_ps[:, g // 32, (g % 32) * H:(g % 32 + 1) * H], q_bd[cp][:, :, g],
                                     k_op[:, cp, :, g], start=True, stop=True)
                last.then_inc(s_sc, 1)

            def prob_transpose(c):
                pe.wait_ge(s_prob, c + 1)
                wait_from_first(pe, s_pt_sb, c)
                for b in range(8):
                    last = pe.transpose(pt_ps[:, b // 4, (b % 4) * P:(b % 4 + 1) * P], prob_f[:, b * P:(b + 1) * P],
                                        ident[:, :])
                last.then_inc(s_pt, 1)

            def value_product(c, cp):
                pe.wait_ge(s_pt_sb, c + 1)
                for t in range(8):
                    for b in range(8):
                        g = 8 * t + b
                        last = pe.matmul(sc_ps[:, g // 32, (g % 32) * H:(g % 32 + 1) * H], v_bd[cp][:, :, g],
                                         prob_t[:, b * P + t * H:b * P + (t + 1) * H], start=True, stop=True)
                last.then_inc(s_pv, 1)

            def pe_step(c, cp, front, proj, attend):
                if attend:
                    scores(c - 2, cp)
                for j in range(TC):
                    t = c * TC + j
                    if front:
                        embed(t, j, cp * TC + j, (c - cp) // 2 + 1)
                    if j > 0 and front:
                        xn_transpose(t - 1, (j - 1) % 2)
                    if j == 0 and proj:
                        xn_transpose(t - 1, 1)
                    if proj:
                        for n in PROJ[j]:
                            project(c - 1, 1 - cp, n)
                if attend:
                    prob_transpose(c - 2)
                    value_product(c - 2, cp)

            embed_chunks(pe, pe_step)

            pe.wait_ge(s_y, 2 * NC)
            pe.wait_ge(s_qkv_sb, 6 * NC)

            def wo_product(t, k):
                pe.wait_ge(t_att, t + 1)
                wait_from_first(pe, t_add, t - 1)
                for h in range(NH2):
                    last = pe.matmul(bank[2 + k][:, 0:E], att_sb[:, k, h, :], wo_sb[:, h, :],
                                     start=(h == 0), stop=(h == NH2 - 1))
                last.then_inc(t_o, 1)

            def xn2_transpose(t, k):
                pe.wait_ge(t_xn, t + 1)
                wait_from_first(pe, t_xT_sb, t - 1)
                for h in range(NH2):
                    last = pe.transpose(bank[k][:, h * P:(h + 1) * P], xn2[:, k, h * P:(h + 1) * P], ident[:, :])
                last.then_inc(t_xT, 1)

            def router(t, k, b):
                pe.wait_ge(t_xT_sb, t + 1)
                wait_from_first(pe, t_lg_sb, t - 1)
                ps = sc_ps[64 * b:64 * b + NX, k, 0:P]
                for h in range(NH2):
                    last = pe.matmul(ps, wr_sb[:, h, :], xn2T[:, k, h * P:(h + 1) * P],
                                     start=(h == 0), stop=(h == NH2 - 1))
                last.then_inc(t_lg, 1)

            wo_product(0, 0)
            for b in range(NB):
                for t, k in ((b * QT + 1, 1),):
                    wo_product(t, k)
                    xn2_transpose(t - 1, 1 - k)
                    router(t - 1, 1 - k, b)
                with pe.Fori(1, QT // 2) as i:
                    for k in range(2):
                        t = b * QT + 2 * i + k
                        wo_product(t, k)
                        xn2_transpose(t - 1, 1 - k)
                        router(t - 1, 1 - k, b)
                if b == 0:
                    wo_product(QT, 0)
                xn2_transpose((b + 1) * QT - 1, 1)
                router((b + 1) * QT - 1, 1, b)

            pe.wait_ge(t_lg_sb, NT)
            pe.wait_ge(c_top, 2)
            pe.transpose(bank[0][:, 0:LP], top[0:LP, :], ident[0:LP, 0:LP]).then_inc(c_T, 1)
            pe.transpose(bank[1][:, 0:LP], top_atf[0:LP, :], ident[0:LP, 0:LP]).then_inc(c_T, 1)
            pe.wait_ge(s_const, 5)
            pe.wait_ge(c_T_sb, 2)
            pe.matmul(bank[2][:, 0:NX], flip[:, :], topT[:, 64:64 + NX], start=True, stop=True)
            pe.matmul(bank[2][:, 64:64 + NX], flip[:, :], topiT[:, 64:64 + NX], start=True, stop=True)
            pe.matmul(bank[2][:, 128:128 + NX], first_row[:, :], topT[:, 0:NX], start=True, stop=True)
            pe.matmul(bank[2][:, 192:192 + NX], first_row[:, :], topT[:, 64:64 + NX], start=True,
                      stop=True).then_inc(c_rev, 1)
            pe.wait_ge(c_exp, 1)
            pe.matmul(bank[3][:, 0:NX], ones[:, :], sel_w[:, :], start=True, stop=True).then_inc(c_sum, 1)

            pe.wait_ge(c_done, 2)
            h_bank = [sc_ps[:, 0, :], sc_ps[:, 1, :], pt_ps[:, 0, :], pt_ps[:, 1, :]]

            def tokens_transpose(e, k, s):
                pe.wait_ge(e_xg[s], 16 * ((e - s) // 4 + 1))
                wait_from_first(pe, e_xgT_sb, e - 1)
                for h in range(NH2):
                    last = pe.transpose(bank[k][:, h * P:(h + 1) * P], xg[:, s, h * P:(h + 1) * P], ident[:, :])
                last.then_inc(e_xgT, 1)

            def up(e, k, s, w_use):
                pe.wait_ge(e_xgT_sb, e + 1)
                pe.wait_ge(e_w[s], 32 * w_use)
                w1 = w_slot[s][:, 0:EW].rearrange("p (h s m) -> p h s m", h=NH2, s=SUB)
                for half in range(2):
                    wait_from_first(pe, e_act, 2 * e + half - 3)
                    for q in range(4):
                        ss, mh = (4 * half + q) // MH, (4 * half + q) % MH
                        for h in range(NH2):
                            last = pe.matmul(h_bank[2 * k + half][:, q * P:(q + 1) * P], w1[:, h, ss, mh * P:(mh + 1) * P],
                                             xgT[:, k, h * P:(h + 1) * P], start=(h == 0), stop=(h == NH2 - 1))
                    last.then_inc(e_h, 1)

            def down(e, k, s):
                w2 = w_slot[s][:, EW:EW + SUB * MH * KO].rearrange("p (s m k) -> p s m k", s=SUB, m=MH)
                pe.wait_ge(e_act, 2 * e + 2)
                wait_from_first(pe, e_yb, e - 1)
                for ss in range(SUB):
                    for mh in range(MH):
                        last = pe.matmul(bank[2 + k][:, ss * KO:(ss + 1) * KO], act[:, k, MH * ss + mh, :], w2[:, ss, mh, :],
                                         start=(mh == 0), stop=(mh == MH - 1))
                last.then_inc(e_y, 1)

            def expert(e, s, w_use):
                tokens_transpose(e, s % 2, s % 4)
                up(e, s % 2, s, w_use)
                if not (isinstance(e, int) and e == 0):
                    down(e - 1, (s + 1) % 2, (s - 1) % WS)

            for e in range(WS):
                expert(e, e, 1)
            with pe.Fori(1, NX // WS) as i:
                for s in range(WS):
                    expert(WS * i + s, s, i + 1)
            down(NX - 1, 1, WS - 1)

        @block.scalar
        def _(sc):
            def h_copy(c, j):
                t, k = c * TC + j, j % 2
                sc.wait_ge(s_h, t + 1)
                wait_from_first(sc, s_xn, t - 1)
                if not (isinstance(c, int) and c == 0 and j < 2):
                    sc.wait_ge(s_h_st[k], 32 * (c * (TC // 2) + j // 2))
                sc.activation(h_sb[:, k, :], bank[k][:, 0:E], ACT.Identity).then_inc(s_h_sb, 1)

            def root(t, k):
                sc.wait_ge(s_mv, t + 1)
                sc.activation(std[:, k:k + 1], mean_var[:, k, 1:2], ACT.Sqrt, bias=eps[:, :]).then_inc(s_std, 1)

            def xT_copy(c, cp, j):
                sc.wait_ge(s_xT, c * TC + j + 1)
                wait_from_first(sc, s_qkv, 6 * (c - 1))
                sc.activation(xnT[:, cp, :, j * P:(j + 1) * P], bank[j % 2][:, 0:E].rearrange("p (h t) -> p h t", h=NH2),
                              ACT.Identity).then_inc(s_xT_sb, 1)

            def bias_add(c, n):
                k = n % 2
                sc.wait_ge(s_qkv, 6 * c + n + 1)
                if not (isinstance(c, int) and c == 0 and n < 2):
                    sc.wait_ge(s_qkv_st[k], 16 * (3 * c + n // 2))
                src, dst = bank[2 + k][:, :], qkv_sb[:, k, :]
                if n // 2 == 2:
                    src = src.rearrange("p (g u) -> p g u", u=8)
                    dst = dst.rearrange("p (u g) -> p g u", u=8)
                sc.activation(dst, src, ACT.Identity, bias=bqkv_sb[:, n:n + 1]).then_inc(s_qkv_sb, 1)

            def exponentials(c):
                sc.wait_ge(s_sub, c + 1)
                sc.activation(prob[:, :, :], prob[:, :, :], ACT.Exp, scale=SCALE).then_inc(s_exp, 1)

            def prob_t_copy(c):
                sc.wait_ge(s_pt, c + 1)
                wait_from_first(sc, s_pv, c)
                sc.activation(prob_t[:, :], pt_ps[:, :, :].rearrange("p a x -> p (a x)"), ACT.Identity).then_inc(s_pt_sb, 1)

            def y_out(c, batch, part):
                sc.wait_ge(s_pv, c + 1)
                pv = sc_ps[:, :, :].rearrange("p a x -> p (a x)").rearrange("p (t w b h) -> p w b t h", w=2, b=8, h=H)
                yv = y_t[:, :, :, :, :].rearrange("p w b h (c q r) -> p w b c q r h", q=8, r=4)
                for w in range(2):
                    dst = yv[:, w, bass.ds(batch, 1), bass.ds(part, 1), :, :, :].rearrange("p b c q r h -> p (b c q) r h")
                    sc.activation(dst, pv[:, w, :, :, :], ACT.Identity).then_inc(s_y, 1)

            def act_step(c, cp, front, proj, attend):
                for j in range(TC):
                    if front:
                        h_copy(c, j)
                        root(c * TC + j, j % 2)
                    if j > 0 and front:
                        xT_copy(c, cp, j - 1)
                    if j == 0 and proj:
                        xT_copy(c - 1, 1 - cp, TC - 1)
                    if proj:
                        for n in PROJ[j]:
                            bias_add(c - 1, n)
                    if attend and j == 1:
                        exponentials(c - 2)
                if attend:
                    prob_t_copy(c - 2)
                    y_out(c - 2, (c - 2) // (NC // NB), (c - 2) % (NC // NB))

            embed_chunks(sc, act_step)

            def root2(t, k):
                sc.wait_ge(t_mv, t + 1)
                sc.activation(std[:, k:k + 1], mean_var[:, k, 1:2], ACT.Sqrt, bias=eps[:, :]).then_inc(t_std, 1)

            def xn2T_copy(t, k):
                sc.wait_ge(t_xT, t + 1)
                wait_from_first(sc, t_lg, t - 1)
                sc.activation(xn2T[:, k, :], bank[k][:, 0:E], ACT.Identity).then_inc(t_xT_sb, 1)

            def logits_out(t, k, b, tt):
                sc.wait_ge(t_lg, t + 1)
                sc.activation(logits[64 * b:64 * b + NX, bass.ds(tt * P, P)], sc_ps[64 * b:64 * b + NX, k, 0:P],
                              ACT.Identity).then_inc(t_lg_sb, 1)

            sc.wait_ge(c_fill, 1)
            root2(0, 0)
            for b in range(NB):
                root2(b * QT + 1, 1)
                xn2T_copy(b * QT, 0)
                logits_out(b * QT, 0, b, 0)
                with sc.Fori(1, QT // 2) as i:
                    for k in range(2):
                        t = b * QT + 2 * i + k
                        root2(t, k)
                        xn2T_copy(t - 1, 1 - k)
                        logits_out(t - 1, 1 - k, b, 2 * i + k - 1)
                if b == 0:
                    root2(QT, 0)
                xn2T_copy((b + 1) * QT - 1, 1)
                logits_out((b + 1) * QT - 1, 1, b, QT - 1)

            sc.wait_ge(c_dve, 8)
            sc.activation(sel_w[:, :], sel_v[:, :], ACT.Exp).then_inc(c_exp, 1)

            sc.wait_ge(c_done, 2)
            h_bank = [sc_ps[:, 0, :], sc_ps[:, 1, :], pt_ps[:, 0, :], pt_ps[:, 1, :]]

            def gelus(e, k):
                for half in range(2):
                    sc.wait_ge(e_h, 2 * e + half + 1)
                    if half == 0:
                        wait_from_first(sc, e_y, e - 1)
                    for q in range(4):
                        n = 4 * half + q
                        last = sc.activation(act[:, k, n, :], h_bank[2 * k + half][:, q * P:(q + 1) * P], ACT.Gelu,
                                             bias=b1_sb[:, bass.ds(e * SUB * MH + n, 1)])
                    last.then_inc(e_act, 1)

            for e in range(2):
                gelus(e, e)
            with sc.Fori(1, NX // 2) as i:
                for k in range(2):
                    gelus(2 * i + k, k)

        @block.vector
        def _(dve):
            for n in range(2):
                dve.memset(q_bd[n][:, :, :], 0.0).then_inc(s_zero, 1)

            def rowsT_copy(t):
                dve.wait_ge(s_rowsT, t // 2 + 1)
                wait_from_first(dve, s_h, t)
                dve.tensor_copy(rowsT[:, :], bank[0][:, 0:P]).then_inc(s_rowsT_sb, 1)

            def norm(src, dst, k, t, m_bn, m_mv, m_std, m_rstd, m_out):
                dve.bn_stats(bn6[:, k, :], src).then_inc(m_bn, 1)
                dve.wait_ge(m_bn, t + 1)
                dve.memset(pad[:, 0:1], 0.0)
                dve.bn_aggr(mean_var[:, k, :], bn6[:, k, :]).then_inc(m_mv, 1)
                dve.wait_ge(m_std, t + 1)
                dve.reciprocal(rstd[:, k:k + 1], std[:, k:k + 1]).then_inc(m_rstd, 1)
                dve.wait_ge(m_rstd, t + 1)
                dve.tensor_scalar(dst, src, mean_var[:, k, 0:1], rstd[:, k:k + 1], ALU.subtract,
                                  ALU.mult).then_inc(m_out, 1)

            def tile_norm(t, k):
                if k == 0:
                    rowsT_copy(t)
                dve.wait_ge(s_h_sb, t + 1)
                wait_from_first(dve, s_xT, t - 1)
                norm(h_sb[:, k, :], xn[:, k, :], k, t, s_bn, s_mv, s_std, s_rstd, s_xn)

            scores_v = sc_ps[:, :, :].rearrange("p a (g h) -> p (a g) h", h=H)

            def less_max(c):
                dve.wait_ge(s_sc, c + 1)
                dve.tensor_reduce(row_max[:, :], scores_v, axis=AX.X, op=ALU.max).then_inc(s_max, 1)
                dve.wait_ge(s_max, c + 1)
                wait_from_first(dve, s_pt, c)
                dve.tensor_tensor(prob[:, :, :], scores_v, row_max[:, :].unsqueeze(2).to_broadcast([P, G, H]),
                                  ALU.subtract).then_inc(s_sub, 1)

            def probabilities(c):
                dve.wait_ge(s_exp, c + 1)
                dve.tensor_reduce(row_sum[:, :], prob[:, :, :], axis=AX.X, op=ALU.add).then_inc(s_sum, 1)
                dve.wait_ge(s_sum, c + 1)
                dve.reciprocal(row_sum[:, :], row_sum[:, :]).then_inc(s_rsum, 1)
                dve.wait_ge(s_rsum, c + 1)
                dve.tensor_tensor(prob[:, :, :], prob[:, :, :], row_sum[:, :].unsqueeze(2).to_broadcast([P, G, H]),
                                  ALU.mult).then_inc(s_prob, 1)

            def dve_step(c, cp, front, proj, attend):
                for j in range(TC):
                    if front:
                        tile_norm(c * TC + j, j % 2)
                    if attend and j == 0:
                        less_max(c - 2)
                    if attend and j == 2:
                        probabilities(c - 2)

            embed_chunks(dve, dve_step)

            dve.wait_ge(s_pv, NC)
            for k in range(2):
                dve.wait_ge(s_h_st[k], 32 * NT // 2)
            dve.memset(logits[0:64, :], LOWEST).then_inc(c_fill, 1)

            def out_tile(t, k):
                dve.wait_ge(t_o, t + 1)
                dve.wait_ge(t_res[k], 16 * ((t - k) // 2 + 1))
                if not (isinstance(t, int) and t < 2):
                    dve.wait_ge(t_h2_st[k], 16 * ((t - k) // 2))
                dve.tensor_tensor(h2_sb[:, k, :], bank[2 + k][:, 0:E], res_sb[:, k, :], ALU.add).then_inc(t_add, 1)
                dve.wait_ge(t_add, t + 1)
                dve.tensor_tensor(h2_sb[:, k, :], h2_sb[:, k, :], bo_sb[:, :], ALU.add).then_inc(t_h2, 1)
                dve.wait_ge(t_h2, t + 1)
                if not (isinstance(t, int) and t < 2):
                    dve.wait_ge(t_xn_st[k], 16 * ((t - k) // 2))
                wait_from_first(dve, t_xT, t - 1)
                norm(h2_sb[:, k, :], xn2[:, k, :], k, t, t_bn, t_mv, t_std, t_rstd, t_xn)

            for k in range(2):
                out_tile(k, k)
            with dve.Fori(1, NT // 2) as i:
                for k in range(2):
                    out_tile(2 * i + k, k)

            dve.wait_ge(t_lg_sb, NT)
            dve.wait_ge(t_att, NT)
            steps = CAP // 8
            top_u = top_at[:, :].bitcast(U32)
            chain = [0]

            def link(ins):
                chain[0] += 1
                ins.then_inc(c_dve, 1)
                dve.wait_ge(c_dve, chain[0])

            c_max = ctx.enter_context(nc.semaphore("c_max"))
            c_rep = ctx.enter_context(nc.semaphore("c_rep"))
            for n in range(steps):
                eight = top[0:LP, 8 * n:8 * n + 8]
                dve.max(eight, logits[0:LP, :]).then_inc(c_max, 1)
                dve.wait_ge(c_max, n + 1)
                dve.max_index(top_u[0:LP, 8 * n:8 * n + 8], eight, logits[0:LP, :]).then_inc(c_rep, 1)
                dve.match_replace(logits[0:LP, :], eight, logits[0:LP, :], LOWEST).then_inc(c_rep, 1)
                dve.wait_ge(c_rep, 2 * n + 2)
            dve.tensor_copy(top_atf[0:LP, :], top_u[0:LP, :]).then_inc(c_top, 1)
            dve.wait_ge(c_top, 1)
            dve.tensor_scalar(top_atf[64:LP, :], top_atf[64:LP, :], float(S), None, ALU.add).then_inc(c_top, 1)
            dve.wait_ge(c_T, 2)
            dve.tensor_copy(topT[:, 0:LP], bank[0][:, 0:LP]).then_inc(c_T_sb, 1)
            dve.tensor_copy(topiT[:, 0:LP], bank[1][:, 0:LP]).then_inc(c_T_sb, 1)
            dve.wait_ge(c_rev, 1)
            dve.wait_ge(c_T_sb, 2)
            link(dve.tensor_tensor(sel_mask[:, :], bank[2][:, 0:NX], topT[:, 0:NX], ALU.is_le))
            link(dve.tensor_tensor(sel_v[:, :], bank[2][:, 0:NX], topT[:, 0:NX], ALU.max))
            link(dve.tensor_copy(sel_max[:, :], bank[2][:, 128:128 + NX]))
            link(dve.tensor_tensor(sel_max[:, :], sel_max[:, :], bank[2][:, 192:192 + NX], ALU.max))
            link(dve.tensor_copy(rev_if[:, :], bank[2][:, 64:64 + NX]))
            link(dve.tensor_tensor(sel_if[:, :], topiT[:, 0:NX], rev_if[:, :], ALU.subtract))
            link(dve.tensor_tensor(sel_if[:, :], sel_if[:, :], sel_mask[:, :], ALU.mult))
            link(dve.tensor_tensor(sel_v[:, :], sel_v[:, :], sel_max[:, :], ALU.subtract))
            dve.tensor_tensor(tok_idx[:, :], sel_if[:, :], rev_if[:, :], ALU.add).then_inc(c_done, 1)
            dve.wait_ge(c_sum, 1)
            link(dve.reciprocal(sel_rden[:, :], bank[3][:, 0:NX]))
            dve.tensor_tensor(sel_w[:, :], sel_w[:, :], sel_rden[:, :], ALU.mult).then_inc(c_done, 1)
            dve.wait_ge(c_done, 2)

            def xgT_copy(e, k):
                dve.wait_ge(e_xgT, e + 1)
                wait_from_first(dve, e_h, 2 * (e - 1))
                dve.tensor_copy(xgT[:, k, :], bank[k][:, 0:E]).then_inc(e_xgT_sb, 1)

            def y_out(e, k, s, use):
                dve.wait_ge(e_y, e + 1)
                if not (isinstance(e, int) and e < 4):
                    dve.wait_ge(e_out, 16 * (e - 3))
                dve.wait_ge(e_b2[s], 16 * use)
                dve.tensor_tensor(y_sb[:, s, :], bank[2 + k][:, 0:E], b2_sb[:, s, :], ALU.add).then_inc(e_yb, 1)
                dve.wait_ge(e_yb, e + 1)
                dve.tensor_scalar(y_sb[:, s, :], y_sb[:, s, :], sel_w[:, bass.ds(e, 1)], None,
                                  ALU.mult).then_inc(e_y_sb, 1)

            xgT_copy(0, 0)
            for e in range(1, 4):
                xgT_copy(e, e % 2)
                y_out(e - 1, (e - 1) % 2, e - 1, 1)
            with dve.Fori(1, NX // 4) as i:
                for s in range(4):
                    e = 4 * i + s
                    xgT_copy(e, s % 2)
                    y_out(e - 1, (s + 1) % 2, (s + 3) % 4, i + (s > 0))
            y_out(NX - 1, 1, 3, NX // 4)


def kernel(x, L0_tok_A, L0_tok_B, L0_attn_Wq, L0_attn_bq, L0_attn_Wk, L0_attn_bk, L0_attn_Wv, L0_attn_bv,
           L0_attn_Wo, L0_attn_bo, L0_ffn_Wr, L0_ffn_W1, L0_ffn_b1, L0_ffn_W2, L0_ffn_b2):
    import numpy as np
    import concourse.bacc as bacc
    from concourse.bass_utils import run_bass_kernel_spmd

    P_ = 128
    c = np.ascontiguousarray
    x, A, B = np.asarray(x), np.asarray(L0_tok_A), np.asarray(L0_tok_B)
    E = B.shape[1]
    W1, W2 = np.asarray(L0_ffn_W1), np.asarray(L0_ffn_W2)
    NX, SUB, _, MID = W1.shape
    K = W2.shape[3]
    arrays = {
        "ids": c(x.reshape(-1, 8, 4, 2, 8).transpose(3, 1, 4, 0, 2)).reshape(P_, -1),
        "A": c(A), "B": c(B),
        "WqT": c(np.asarray(L0_attn_Wq).T), "WkT": c(np.asarray(L0_attn_Wk).T),
        "WvT": c(np.asarray(L0_attn_Wv).T), "WoT": c(np.asarray(L0_attn_Wo).T),
        "bqkv": c(np.concatenate([np.asarray(v).reshape(-1, P_) for v in (L0_attn_bq, L0_attn_bk, L0_attn_bv)]).T),
        "bo": c(np.asarray(L0_attn_bo).reshape(1, E)),
        "WrT": c(np.asarray(L0_ffn_Wr).T),
        "W1": c(W1.reshape(NX, SUB, E // P_, P_, MID).transpose(0, 3, 2, 1, 4)).reshape(NX, P_, -1),
        "b1T": c(np.asarray(L0_ffn_b1).reshape(-1, P_).T),
        "W2": c(W2.reshape(NX, SUB, MID // P_, P_, K).transpose(0, 3, 1, 2, 4)).reshape(NX, P_, -1),
        "b2": c(np.asarray(L0_ffn_b2).reshape(NX, E)),
    }
    nc = bacc.Bacc("TRN2", target_bir_lowering=False, num_devices=1)
    args = [nc.dram_tensor(n, a.shape, mybir.dt.from_np(a.dtype), kind="ExternalInput").ap() for n, a in arrays.items()]
    args.append(nc.dram_tensor("out", (x.size, E), F32, kind="ExternalOutput").ap())
    tower_kernel(nc, *args)
    r = run_bass_kernel_spmd(nc, [arrays], core_ids=[0])
    return r.results[0]["out"].reshape(*x.shape, E)
```

```python
from contextlib import ExitStack

import concourse.bass as bass
from concourse import mybir

P = 128
F32 = mybir.dt.float32
BF16 = mybir.dt.bfloat16
I32 = mybir.dt.int32
U32 = mybir.dt.uint32
ALU = mybir.AluOpType
ACT = mybir.ActivationFunctionType
AX = mybir.AxisListType
LN_EPS = 1e-5
LOWEST = -3.0e38


def wait_from_first(eng, sem, count):
    if isinstance(count, int) and count <= 0:
        return
    eng.wait_ge(sem, count)


def tower_kernel(nc, ids, A, B, WqT, WkT, WvT, WoT, bqkv, bo, WrT, W1, b1T, W2, b2, out):
    RANK, E = B.shape
    NX, _, EW = W1.shape
    T = ids.shape[0] * ids.shape[1]
    NB, S = 2, T // 2
    NT = T // P
    H, D = 16, E // 16
    NH2 = E // P
    CH = 512
    TC = CH // P
    NC = T // CH
    QT = S // P
    SUB = 4
    MID = EW // (NH2 * SUB)
    MH = MID // P
    KO = E // SUB
    CAP = int(1.5 * T / NX)
    SCALE = 1.0 / float(D) ** 0.5
    G = CH // 8
    assert CAP == P and NB * NX <= P and NC % 2 == 0 and G == 64 and 8 * D == P and H == D

    h_dram = nc.dram_tensor("h_dram", [T, E], F32).ap()
    qkv_dram = nc.dram_tensor("qkv_dram", [NC, 3, E, CH], F32).ap()
    xn_dram = nc.dram_tensor("xn_dram", [T, E], F32).ap()

    ctx = ExitStack()
    with ctx:
        def sb(name, shape, dt=F32):
            return ctx.enter_context(nc.sbuf_tensor(name, shape, dt))

        def sem(name):
            return ctx.enter_context(nc.semaphore(name))

        big = sb("big", [P, 4 * P * G])
        k_bd = [big[:, n * P * G:(n + 1) * P * G].rearrange("p (m g) -> p m g", g=G) for n in (0, 1)]
        v_bd = [big[:, n * P * G:(n + 1) * P * G].rearrange("p (m g) -> p m g", g=G) for n in (2, 3)]
        WN = EW + SUB * MH * KO
        WB = 4
        WS = 12
        w_slot = [big[:, s * WN:(s + 1) * WN] for s in range(WS)]
        q_op = sb("q_op", [P, H, G])
        y_t = sb("y_t", [P, NH2, NB, H, P])
        work = sb("work", [P, 5760])
        ident = sb("ident", [P, P])
        eps = sb("eps", [P, 1])
        pad = sb("pad", [P, 2])
        ids_sb = sb("ids_sb", [P, NT], I32)
        b_sb = sb("b_sb", [P, 2 * E])
        bqkv_sb = sb("bqkv_sb", [P, 3 * NH2])
        wo_sb = sb("wo_sb", [P, NH2, E])
        wr_sb = sb("wr_sb", [P, NH2, NX])
        bn6 = sb("bn6", [P, 2, 6])
        mean_var = sb("mean_var", [P, 2, 2])
        std = sb("std", [P, 2])
        rstd = sb("rstd", [P, 2])
        rows_sb = sb("rows_sb", [P, 2 * TC, RANK])

        def carve(base, at, n):
            return base[:, at:at + n], at + n

        at = 0
        wqkv_sb, at = carve(work, at, 3 * NH2 * E)
        wqkv_sb = wqkv_sb.rearrange("p (w h e) -> p w h e", w=3, h=NH2)
        xnT, at = carve(work, at, 2 * NH2 * CH)
        xnT = xnT.rearrange("p (k h t) -> p k h t", k=2, h=NH2)
        rowsT, at = carve(work, at, P)
        h_sb, at = carve(work, at, 2 * E)
        h_sb = h_sb.rearrange("p (k e) -> p k e", k=2)
        xn, at = carve(work, at, 2 * E)
        xn = xn.rearrange("p (k e) -> p k e", k=2)
        NR = G // 8 * 8
        prob = sb("prob", [P, 2, NR, H])
        prob_t = sb("prob_t", [P, G * H + 1])
        prob_t_at = (0, G * H // 2 + 1)
        row_max = sb("row_max", [P, 2, NR])
        row_sum = sb("row_sum", [P, 2, NR])
        qkv_sb, at = carve(work, at, 2 * CH)
        qkv_sb = qkv_sb.rearrange("p (k t) -> p k t", k=2)
        assert at <= 5760
        at = 0
        res_sb, at = carve(work, at, 4 * E)
        h2_sb, at = carve(work, at, 4 * E)
        xn2, at = carve(work, at, 4 * E)
        res_sb, h2_sb, xn2 = (v.rearrange("p (k n e) -> p k n e", k=2, n=2) for v in (res_sb, h2_sb, xn2))
        xn2T, at = carve(work, at, 2 * E)
        xn2T = xn2T.rearrange("p (h t) -> p h t", h=NH2)
        prob_f = prob[:, :, :, :].rearrange("p a g h -> p (a g h)")
        bo_sb, _ = carve(prob_f, 4 * E, E)
        att_sb = prob_f[:, 0:4 * E].rearrange("p (k h n r) -> p k h n r", k=2, h=NH2, n=2)
        logits, at = carve(work, at, S)
        LP = 64 + NX
        assert at <= 5760
        y_flat = y_t[:, :, :, :, :].rearrange("p w b h r -> p (w b h r)")
        at = 0
        top, at = carve(y_flat, at, CAP)
        top_at, at = carve(y_flat, at, CAP)
        top_atf, at = carve(y_flat, at, CAP)
        topT, at = carve(y_flat, at, P)
        topiT, at = carve(y_flat, at, P)
        b2_sb, at = carve(y_flat, at, WB * E)
        b2_sb = b2_sb.rearrange("p (k e) -> p k e", k=WB)
        b1_sb, at = carve(y_flat, at, NX * SUB * MH)
        flip, at = carve(y_flat, at, P)
        first_row, at = carve(y_flat, at, P)
        ones, at = carve(y_flat, at, P)
        sel_mask, at = carve(y_flat, at, NX)
        sel_v, at = carve(y_flat, at, NX)
        sel_max, at = carve(y_flat, at, NX)
        sel_w, at = carve(y_flat, at, NX)
        sel_if, at = carve(y_flat, at, NX)
        sel_rden, at = carve(y_flat, at, NX)
        rev_if, at = carve(y_flat, at, NX)
        tok_idx, at = carve(y_flat, at, NX)
        tok_idx = tok_idx.bitcast(I32)
        at = 0
        xg, at = carve(work, at, 4 * E)
        xg = xg.rearrange("p (k e) -> p k e", k=4)
        xgT, at = carve(work, at, 2 * E)
        xgT = xgT.rearrange("p (k e) -> p k e", k=2)
        act, at = carve(work, at, 2 * SUB * MH * P)
        act = act.rearrange("p (k s t) -> p k s t", k=2, t=P)
        y_sb, at = carve(work, at, 4 * E)
        y_sb = y_sb.rearrange("p (k e) -> p k e", k=4)
        assert at <= 5760

        bank = [ctx.enter_context(nc.psum_tensor(f"bank{i}", [P, CH], F32)) for i in range(4)]
        att_ps = ctx.enter_context(nc.psum_tensor("att_ps", [P, 4, CH], F32))

        s_const = sem("s_const")
        s_id = sem("s_id")
        s_zero = sem("s_zero")
        s_bzero = sem("s_bzero")
        s_ids = sem("s_ids")
        s_w = sem("s_w")
        s_rows = [sem(f"s_rows{k}") for k in range(8)]
        s_rowsT = sem("s_rowsT")
        s_rowsT_sb = sem("s_rowsT_sb")
        s_h = sem("s_h")
        s_h_sb = sem("s_h_sb")
        s_h_st = sem("s_h_st")
        s_bn = sem("s_bn")
        s_mv = sem("s_mv")
        s_std = sem("s_std")
        s_rstd = sem("s_rstd")
        s_xn = sem("s_xn")
        s_xT = sem("s_xT")
        s_xT_sb = sem("s_xT_sb")
        s_qkv = sem("s_qkv")
        s_qkv_sb = sem("s_qkv_sb")
        s_qkv_st = [sem(f"s_qkv_st{k}") for k in range(2)]
        s_qk = [sem(f"s_qk{k}") for k in range(2)]
        s_v = [sem(f"s_v{k}") for k in range(2)]
        s_sc = sem("s_sc")
        s_max = sem("s_max")
        s_sub = sem("s_sub")
        s_exp = sem("s_exp")
        s_sum = sem("s_sum")
        s_rsum = sem("s_rsum")
        s_pt = sem("s_pt")
        s_pt_sb = sem("s_pt_sb")
        s_pv = sem("s_pv")
        s_o = sem("s_o")
        s_ot = sem("s_ot")
        s_y = sem("s_y")
        s_bo = sem("s_bo")
        t_att = sem("t_att")
        t_res = [sem(f"t_res{k}") for k in range(2)]
        t_res_b = sem("t_res_b")
        t_o = sem("t_o")
        t_h2 = sem("t_h2")
        t_h2_st = [sem(f"t_h2_st{k}") for k in range(2)]
        t_bn = sem("t_bn")
        t_mv = sem("t_mv")
        t_std = sem("t_std")
        t_rstd = sem("t_rstd")
        t_xn = sem("t_xn")
        t_xn_st = [sem(f"t_xn_st{k}") for k in range(2)]
        t_xT = sem("t_xT")
        t_xT_sb = sem("t_xT_sb")
        t_lg = sem("t_lg")
        t_lg_sb = sem("t_lg_sb")
        s_b1 = sem("s_b1")
        c_fill = sem("c_fill")
        c_top = sem("c_top")
        c_T = sem("c_T")
        c_T_sb = sem("c_T_sb")
        c_rev = sem("c_rev")
        c_dve = sem("c_dve")
        c_exp = sem("c_exp")
        c_sum = sem("c_sum")
        c_done = sem("c_done")
        e_w = [sem(f"e_w{k}") for k in range(WS)]
        e_b2 = [sem(f"e_b2{k}") for k in range(WB)]
        e_xg = [sem(f"e_xg{k}") for k in range(4)]
        e_xgT = sem("e_xgT")
        e_xgT_sb = sem("e_xgT_sb")
        e_h = sem("e_h")
        e_act = sem("e_act")
        e_y = sem("e_y")
        e_yb = sem("e_yb")
        e_y_sb = sem("e_y_sb")
        e_out = sem("e_out")

        block = ctx.enter_context(nc.Block())

        def load_weights(eng, e, s):
            eng.dma_start(w_slot[s][:, 0:EW], W1[bass.ds(e, 1), :, :].rearrange("a p n -> (a p) n")).then_inc(e_w[s], 16)
            eng.dma_start(w_slot[s][:, EW:WN], W2[bass.ds(e, 1), :, :].rearrange("a p n -> (a p) n")).then_inc(e_w[s], 16)

        def embed_chunks(eng, step):
            for c in range(4):
                step(c, c % 2, True, c >= 1, c >= 2)
            with eng.Fori(2, NC // 2) as i:
                for u in range(2):
                    step(2 * i + u, u, True, True, True)
            step(NC, 0, False, True, True)
            step(NC + 1, 1, False, False, True)

        @block.sync
        def _(sp):
            sp.dma_start(ids_sb[:, :], ids).then_inc(s_ids, 16)
            sp.wait_ge(s_bzero, 1)
            for k in range(2):
                sp.dma_start(b_sb[k * RANK:(k + 1) * RANK, k * E:(k + 1) * E], B).then_inc(s_w, 16)
            for n, w in enumerate((WqT, WkT, WvT)):
                sp.dma_start(wqkv_sb[:, n, :, :], w.rearrange("(h p) e -> p h e", p=P)).then_inc(s_w, 16)
            sp.dma_start(bqkv_sb[:, :], bqkv).then_inc(s_w, 16)
            sp.dma_start(wo_sb[:, :, :], WoT.rearrange("(h p) e -> p h e", p=P)).then_inc(s_w, 16)
            sp.dma_start(wr_sb[:, :, :], WrT.rearrange("(h p) e -> p h e", p=P)).then_inc(s_w, 16)

            h_rows = h_dram.rearrange("(c g u) e -> c g u e", g=G, u=8)

            def store_h(c, j):
                sp.wait_ge(s_h_sb, 2 * c + j + 1)
                for v in range(2):
                    sp.dma_start(h_rows[bass.ds(c, 1), :, 4 * j + v:4 * j + 4:2, :].rearrange("c g k e -> (c g) k e"),
                                 h_sb[G * v:G * v + G, :, :]).then_inc(s_h_st, 16)

            def store_qkv(c, n):
                sp.wait_ge(s_qkv_sb, 6 * c + n + 1)
                sp.dma_start(qkv_dram[bass.ds(c, 1), n // 2, (n % 2) * P:(n % 2) * P + P, :]
                             .rearrange("c f t -> (c f) t"), qkv_sb[:, n % 2, :]).then_inc(s_qkv_st[n % 2], 16)

            def operand_source(c, w, t):
                return qkv_dram[bass.ds(c, 1), w, :, G * t:G * t + G]

            def load_qk(c, cp):
                sp.wait_ge(s_qkv_st[0], 48 * c + 32)
                sp.wait_ge(s_qkv_st[1], 48 * c + 32)
                for u in range(8):
                    r = slice(D * u, D * u + D)
                    sp.dma_start(k_bd[cp][r, H * u:H * u + H, :],
                                 operand_source(c, 1, u).rearrange("c (h d) g -> (c d) h g", d=D)).then_inc(s_qk[cp], 16)
                wait_from_first(sp, s_sc, 2 * c)
                for u in range(8):
                    sp.dma_start(q_op[D * u:D * u + D, :, :],
                                 operand_source(c, 0, u).rearrange("c (h d) g -> (c d) h g", d=D)).then_inc(s_qk[cp], 16)
                    if u == 0:
                        wait_from_first(sp, s_pv, 2 * (c - 1))

            def load_v(c, cp):
                sp.wait_ge(s_qkv_st[0], 48 * (c + 1))
                sp.wait_ge(s_qkv_st[1], 48 * (c + 1))
                for u in range(8):
                    sp.dma_start(v_bd[cp][H * u:H * u + H, D * u:D * u + D, :],
                                 operand_source(c, 2, u).rearrange("c (h d) g -> (c h) d g", d=D)).then_inc(s_v[cp], 16)

            def sp_step(c, cp, front, project, attend):
                if isinstance(c, int) and c == 1:
                    sp.wait_ge(s_zero, 5)
                if front:
                    store_h(c, 0)
                if project:
                    for n in range(4):
                        store_qkv(c - 1, n)
                    load_qk(c - 1, 1 - cp)
                if front:
                    store_h(c, 1)
                if project:
                    for n in range(4, 6):
                        store_qkv(c - 1, n)
                    load_v(c - 1, 1 - cp)

            embed_chunks(sp, sp_step)

            sp.wait_ge(s_y, 2 * NC)
            sp.dma_start(bo_sb[:, :], bo.to_broadcast([P, E])).then_inc(s_bo, 16)
            for s in range(WS):
                sp.dma_start(w_slot[s][:, 0:EW], W1[s, :, :]).then_inc(e_w[s], 16)
                sp.dma_start(w_slot[s][:, EW:WN], W2[s, :, :]).then_inc(e_w[s], 16)

            sp.wait_ge(s_h_st, 32 * NT // 2)

            def load_res(p, k):
                wait_from_first(sp, t_h2, p - 1)
                sp.dma_start(res_sb[:, k, :, :], h_dram[bass.ds(p * 2 * P, 2 * P), :].rearrange("(n p) e -> p n e", p=P)
                             ).then_inc(t_res[k], 16)

            def store_pair(p, k):
                sp.wait_ge(t_h2, p + 1)
                sp.dma_start(out[bass.ds(p * 2 * P, 2 * P), :].rearrange("(n p) e -> p n e", p=P), h2_sb[:, k, :, :]
                             ).then_inc(t_h2_st[k], 16)
                sp.wait_ge(t_xn, p + 1)
                sp.dma_start(xn_dram[bass.ds(p * 2 * P, 2 * P), :].rearrange("(n p) e -> p n e", p=P), xn2[:, k, :, :]
                             ).then_inc(t_xn_st[k], 16)

            load_res(0, 0)
            load_res(1, 1)
            for k in range(2):
                store_pair(k, k)
                load_res(k + 2, k)
            with sp.Fori(1, NT // 4 - 1) as i:
                for k in range(2):
                    store_pair(2 * i + k, k)
                    load_res(2 * i + k + 2, k)
            for k in range(2):
                store_pair(NT // 2 - 2 + k, k)

            sp.wait_ge(t_att, NT // 2)
            sp.dma_start(b1_sb[:, :], b1T).then_inc(s_b1, 16)
            for e in range(WB):
                sp.dma_start(b2_sb[:, e, :], b2[e:e + 1, :].to_broadcast([P, E])).then_inc(e_b2[e], 16)

            def refill(e, s):
                new = sp.snap(e + WS)
                """Expert e + WS's weights and expert e + WB's bias, in the place of expert e's."""
                sp.wait_ge(e_y, e + 1)
                load_weights(sp, new, s)
                refill_bias(e, s)

            def refill_bias(e, s):
                sp.wait_ge(e_yb, e + 1)
                sp.dma_start(b2_sb[:, s % WB, :], b2[bass.ds(e + WB, 1), :].to_broadcast([P, E])
                             ).then_inc(e_b2[s % WB], 16)

            with sp.Fori(0, NX // WS - 1) as i:
                for s in range(WS):
                    refill(i * WS + s, s)
            for s in range(WS - WB):
                refill_bias(NX - WS + s, s)
            sp.wait_ge(e_out, 16 * NX)

        @block.gpsimd
        def _(pool):
            pool.memset(ident[:, :], 0.0).then_inc(s_id, 1)
            pool.memset(eps[:, :], LN_EPS).then_inc(s_const, 1)
            pool.wait_ge(s_id, 1)
            pool.affine_select(out=ident[:, :], in_=ident[:, :], compare_op=ALU.not_equal, fill=1.0,
                               base=0, pattern=[[-1, P]], channel_multiplier=1).then_inc(s_const, 1)
            for n in range(2):
                pool.memset(v_bd[n][:, :, :], 0.0).then_inc(s_zero, 1)

            pool.wait_ge(s_ids, 16)
            for t in range(NT):
                k = t % (2 * TC)
                if t >= 2 * TC:
                    pool.wait_ge(s_rowsT, (t - 2 * TC) // 2 + 1)
                pool.indirect_dma_start(out=rows_sb[:, k, :], out_offset=None, in_=A,
                                        in_offset=bass.IndirectOffsetOnAxis(ap=ids_sb[:, t:t + 1], axis=0)
                                        ).then_inc(s_rows[k], 16)

            pool.wait_ge(s_y, 2 * NC)

            def lay_pair(p, b, pp, k):
                wait_from_first(pool, t_o, p - 1)
                pool.tensor_copy(att_sb[:, k, :, :, :].rearrange("p h n r -> p h (n r)"),
                                 y_t[:, :, bass.ds(b, 1), bass.ds(2 * pp, 2), :].rearrange("p h b n r -> p h (b n r)")
                                 ).then_inc(t_att, 1)

            def bias_pair(p, k):
                pool.wait_ge(t_res[k], 16 * ((p - k) // 2 + 1))
                pool.tensor_tensor(res_sb[:, k, :, :], res_sb[:, k, :, :], bo_sb[:, :].unsqueeze(1).to_broadcast([P, 2, E]),
                                   ALU.add).then_inc(t_res_b, 1)

            pool.wait_ge(s_bo, 16)
            for k in range(2):
                lay_pair(k, 0, k, k)
                bias_pair(k, k)
            with pool.Fori(1, NT // 4) as i:
                for k in range(2):
                    p = 2 * i + k
                    lay_pair(p, p // (QT // 2), p % (QT // 2), k)
                    bias_pair(p, k)

            pool.wait_ge(t_att, NT // 2)
            pool.memset(flip[:, :], 0.0).then_inc(s_id, 1)
            pool.memset(first_row[:, :], 0.0).then_inc(s_id, 1)
            pool.memset(ones[:, :], 1.0).then_inc(s_const, 1)
            pool.wait_ge(s_id, 3)
            pool.affine_select(out=flip[:, :], in_=flip[:, :], compare_op=ALU.not_equal, fill=1.0,
                               base=1 - P, pattern=[[1, P]], channel_multiplier=1).then_inc(s_const, 1)
            pool.affine_select(out=first_row[:, :], in_=first_row[:, :], compare_op=ALU.not_equal, fill=1.0,
                               base=0, pattern=[[0, P]], channel_multiplier=1).then_inc(s_const, 1)

            pool.wait_ge(c_done, 2)
            for k in range(2):
                pool.wait_ge(t_xn_st[k], 16 * NT // 4)
                pool.wait_ge(t_h2_st[k], 16 * NT // 4)

            def fetch(e):
                if e >= 4:
                    pool.wait_ge(e_xgT, e - 3)
                pool.indirect_dma_start(out=xg[:, e % 4, :], out_offset=None, in_=xn_dram,
                                        in_offset=bass.IndirectOffsetOnAxis(ap=tok_idx[:, e:e + 1], axis=0)
                                        ).then_inc(e_xg[e % 4], 16)

            def add_out(e):
                pool.wait_ge(e_y_sb, e + 1)
                if e > 0:
                    pool.wait_ge(e_out, 16 * e)
                pool.indirect_dma_start(out=out, out_offset=bass.IndirectOffsetOnAxis(ap=tok_idx[:, e:e + 1], axis=0),
                                        in_=y_sb[:, e % 4, :], in_offset=None, compute_op=ALU.add).then_inc(e_out, 16)

            for e in range(NX + 2):
                if e < NX:
                    fetch(e)
                if e >= 2:
                    add_out(e - 2)

        @block.tensor
        def _(pe):
            pe.wait_ge(s_const, 2)
            pe.wait_ge(s_w, 16 * 8)

            def rows_transpose(c, cp, j):
                slot = cp * TC + 2 * j
                pe.wait_ge(s_rows[slot], 16 * ((c - cp) // 2 + 1))
                pe.wait_ge(s_rows[slot + 1], 16 * ((c - cp) // 2 + 1))
                wait_from_first(pe, s_h_sb, 2 * c + j)
                pe.transpose(bank[0][:, 0:P], rows_sb[:, slot:slot + 2, :].rearrange("p k r -> p (k r)"),
                             ident[:, :]).then_inc(s_rowsT, 1)

            def embed(c, j):
                pe.wait_ge(s_rowsT_sb, 2 * c + j + 1)
                pe.matmul(bank[0][:, :], rowsT[:, :], b_sb[:, :], start=True, stop=True).then_inc(s_h, 1)

            def xn_transpose(c, j):
                pe.wait_ge(s_xn, 2 * c + j + 1)
                wait_from_first(pe, s_xT_sb, 2 * c + j)
                for h in range(NH2):
                    for k in range(2):
                        last = pe.transpose(bank[1][:, (2 * h + k) * P:(2 * h + k + 1) * P],
                                            xn[:, k, h * P:(h + 1) * P], ident[:, :])
                last.then_inc(s_xT, 1)

            def project(c, cp, n):
                if n == 0:
                    pe.wait_ge(s_xT_sb, 2 * c + 2)
                wait_from_first(pe, s_qkv_sb, 6 * c + n - 1)
                f = (n % 2) * P
                for h in range(NH2):
                    last = pe.matmul(bank[2 + n % 2][:, :], wqkv_sb[:, n // 2, h, f:f + P], xnT[:, cp, h, :],
                                     start=(h == 0), stop=(h == NH2 - 1))
                last.then_inc(s_qkv, 1)

            def block(half, b):
                return 2 * half + b // 4, slice((b % 4) * P, (b % 4 + 1) * P)

            def scores(c, cp, half):
                if half == 0:
                    pe.wait_ge(s_qk[cp], 16 * 16 * ((c - cp) // 2 + 1))
                wait_from_first(pe, s_y, 2 * (c - 1) + half + 1)
                q_pairs = q_op[:, :, :].rearrange("p h (a g) -> p (h a) g", a=2)
                for b in range(8):
                    bk, cols = block(half, b)
                    for q in range(4):
                        g = 32 * half + 4 * b + q
                        last = pe.matmul(att_ps[32 * q:32 * q + 32, bk, cols], q_pairs[:, :, g - 32 * half], k_bd[cp][:, :, g],
                                         start=True, stop=True)
                last.then_inc(s_sc, 1)

            def prob_transpose(c, half):
                pe.wait_ge(s_exp, 2 * c + half + 1)
                for b in range(8):
                    bk, cols = block(half, b)
                    last = pe.transpose(att_ps[:, bk, cols], prob_f[:, (8 * half + b) * P:(8 * half + b + 1) * P], ident[:, :])
                last.then_inc(s_pt, 1)

            def value_product(c, cp, half):
                if half == 0:
                    pe.wait_ge(s_v[cp], 16 * 8 * ((c - cp) // 2 + 1))
                pe.wait_ge(s_pt_sb, 2 * c + half + 1)
                for b in range(8):
                    bk, cols = block(half, b)
                    for q in range(4):
                        g = 32 * half + 4 * b + q
                        at = prob_t_at[half] + 32 * ((4 * b + q) // 2) + q % 2 - half
                        last = pe.matmul(att_ps[32 * q:32 * q + 32, bk, cols], prob_t[:, at:at + 32], v_bd[cp][:, :, g],
                                         start=True, stop=True)
                last.then_inc(s_pv, 1)

            def out_transpose(c, half):
                pe.wait_ge(s_o, 2 * c + half + 1)
                for b in range(8):
                    bk, cols = block(half, b)
                    last = pe.transpose(att_ps[:, bk, cols], prob_f[:, (8 * half + b) * P:(8 * half + b + 1) * P], ident[:, :])
                last.then_inc(s_ot, 1)

            def pe_step(c, cp, front, proj, attend):
                if front:
                    rows_transpose(c, cp, 0)
                if proj:
                    xn_transpose(c - 1, 1)
                if front:
                    embed(c, 0)
                if proj:
                    project(c - 1, 1 - cp, 0)
                    project(c - 1, 1 - cp, 1)
                if attend:
                    scores(c - 2, cp, 0)
                    scores(c - 2, cp, 1)
                if front:
                    rows_transpose(c, cp, 1)
                    xn_transpose(c, 0)
                    embed(c, 1)
                if proj:
                    project(c - 1, 1 - cp, 2)
                for half in range(2):
                    if attend:
                        prob_transpose(c - 2, half)
                if proj:
                    project(c - 1, 1 - cp, 3)
                for half in range(2):
                    if attend:
                        value_product(c - 2, cp, half)
                if proj:
                    project(c - 1, 1 - cp, 4)
                for half in range(2):
                    if attend:
                        out_transpose(c - 2, half)
                if proj:
                    project(c - 1, 1 - cp, 5)

            embed_chunks(pe, pe_step)

            pe.wait_ge(s_y, 2 * NC)
            pe.wait_ge(s_qkv_sb, 6 * NC)

            def wo_product(p, k):
                pe.wait_ge(t_att, p + 1)
                wait_from_first(pe, t_h2, p - 1)
                for n in range(2):
                    for h in range(NH2):
                        last = pe.matmul(bank[2 + k][:, n * E:(n + 1) * E], att_sb[:, k, h, n, :], wo_sb[:, h, :],
                                         start=(h == 0), stop=(h == NH2 - 1))
                last.then_inc(t_o, 1)

            def xn2_transpose(p, k):
                pe.wait_ge(t_xn, p + 1)
                wait_from_first(pe, t_xT_sb, p - 1)
                for h in range(NH2):
                    for n in range(2):
                        last = pe.transpose(bank[k][:, (2 * h + n) * P:(2 * h + n + 1) * P],
                                            xn2[:, k, n, h * P:(h + 1) * P], ident[:, :])
                last.then_inc(t_xT, 1)

            def router(p, k, b):
                pe.wait_ge(t_xT_sb, p + 1)
                wait_from_first(pe, t_lg_sb, p - 1)
                for h in range(NH2):
                    last = pe.matmul(att_ps[64 * b:64 * b + NX, k, 0:2 * P], wr_sb[:, h, :], xn2T[:, h, :],
                                     start=(h == 0), stop=(h == NH2 - 1))
                last.then_inc(t_lg, 1)

            HP = QT // 2
            wo_product(0, 0)
            wo_product(1, 1)
            for k in range(2):
                xn2_transpose(k, k)
                wo_product(k + 2, k)
                router(k, k, 0)
            with pe.Fori(1, HP // 2) as i:
                for k in range(2):
                    xn2_transpose(2 * i + k, k)
                    wo_product(2 * i + k + 2, k)
                    router(2 * i + k, k, 0)
            with pe.Fori(HP // 2, HP - 1) as i:
                for k in range(2):
                    xn2_transpose(2 * i + k, k)
                    wo_product(2 * i + k + 2, k)
                    router(2 * i + k, k, 1)
            for k in range(2):
                xn2_transpose(NT // 2 - 2 + k, k)
                router(NT // 2 - 2 + k, k, 1)

            pe.wait_ge(t_lg_sb, NT // 2)
            pe.wait_ge(c_top, 2)
            pe.transpose(bank[0][:, 0:LP], top[0:LP, :], ident[0:LP, 0:LP]).then_inc(c_T, 1)
            pe.transpose(bank[1][:, 0:LP], top_atf[0:LP, :], ident[0:LP, 0:LP]).then_inc(c_T, 1)
            pe.wait_ge(s_const, 5)
            pe.wait_ge(c_T_sb, 2)
            pe.matmul(bank[2][:, 0:NX], flip[:, :], topT[:, 64:64 + NX], start=True, stop=True)
            pe.matmul(bank[2][:, 64:64 + NX], flip[:, :], topiT[:, 64:64 + NX], start=True, stop=True)
            pe.matmul(bank[2][:, 128:128 + NX], first_row[:, :], topT[:, 0:NX], start=True, stop=True)
            pe.matmul(bank[2][:, 192:192 + NX], first_row[:, :], topT[:, 64:64 + NX], start=True,
                      stop=True).then_inc(c_rev, 1)
            pe.wait_ge(c_exp, 1)
            pe.matmul(bank[3][:, 0:NX], ones[:, :], sel_w[:, :], start=True, stop=True).then_inc(c_sum, 1)

            pe.wait_ge(c_done, 2)
            h_bank = [att_ps[:, n, :] for n in range(4)]

            def tokens_transpose(e, k, s):
                pe.wait_ge(e_xg[s], 16 * ((e - s) // 4 + 1))
                wait_from_first(pe, e_xgT_sb, e - 1)
                for h in range(NH2):
                    last = pe.transpose(bank[k][:, h * P:(h + 1) * P], xg[:, s, h * P:(h + 1) * P], ident[:, :])
                last.then_inc(e_xgT, 1)

            def up(e, k, s, w_use):
                pe.wait_ge(e_xgT_sb, e + 1)
                pe.wait_ge(e_w[s], 32 * w_use)
                w1 = w_slot[s][:, 0:EW].rearrange("p (h s m) -> p h s m", h=NH2, s=SUB)
                for half in range(2):
                    wait_from_first(pe, e_act, 2 * e + half - 3)
                    for q in range(4):
                        ss, mh = (4 * half + q) // MH, (4 * half + q) % MH
                        for h in range(NH2):
                            last = pe.matmul(h_bank[2 * k + half][:, q * P:(q + 1) * P], w1[:, h, ss, mh * P:(mh + 1) * P],
                                             xgT[:, k, h * P:(h + 1) * P], start=(h == 0), stop=(h == NH2 - 1))
                    last.then_inc(e_h, 1)

            def down(e, k, s):
                w2 = w_slot[s][:, EW:EW + SUB * MH * KO].rearrange("p (s m k) -> p s m k", s=SUB, m=MH)
                pe.wait_ge(e_act, 2 * e + 2)
                wait_from_first(pe, e_yb, e - 1)
                for ss in range(SUB):
                    for mh in range(MH):
                        last = pe.matmul(bank[2 + k][:, ss * KO:(ss + 1) * KO], act[:, k, MH * ss + mh, :], w2[:, ss, mh, :],
                                         start=(mh == 0), stop=(mh == MH - 1))
                last.then_inc(e_y, 1)

            def expert(e, s, w_use):
                tokens_transpose(e, s % 2, s % 4)
                up(e, s % 2, s, w_use)
                if not (isinstance(e, int) and e == 0):
                    down(e - 1, (s + 1) % 2, (s - 1) % WS)

            for e in range(WS):
                expert(e, e, 1)
            with pe.Fori(1, NX // WS) as i:
                for s in range(WS):
                    expert(WS * i + s, s, i + 1)
            down(NX - 1, 1, WS - 1)

        @block.scalar
        def _(sc):
            def h_copy(c, j):
                sc.wait_ge(s_h, 2 * c + j + 1)
                wait_from_first(sc, s_xn, 2 * c + j)
                wait_from_first(sc, s_h_st, 32 * (2 * c + j))
                sc.activation(h_sb[:, :, :].rearrange("p k e -> p (k e)"), bank[0][:, :], ACT.Identity).then_inc(s_h_sb, 1)

            def root(c, j):
                sc.wait_ge(s_mv, 4 * c + 2 * j + 2)
                sc.activation(std[:, :], mean_var[:, :, 1], ACT.Sqrt, bias=eps[:, :]).then_inc(s_std, 1)

            def xT_copy(c, cp, j):
                sc.wait_ge(s_xT, 2 * c + j + 1)
                wait_from_first(sc, s_qkv, 6 * (c - 1))
                sc.activation(xnT[:, cp, :, j * 2 * P:(j + 1) * 2 * P], bank[1][:, :].rearrange("p (h t) -> p h t", h=NH2),
                              ACT.Identity).then_inc(s_xT_sb, 1)

            def bias_add(c, n):
                k = n % 2
                sc.wait_ge(s_qkv, 6 * c + n + 1)
                if not (isinstance(c, int) and c == 0 and n < 2):
                    sc.wait_ge(s_qkv_st[k], 16 * (3 * c + n // 2))
                sc.activation(qkv_sb[:, k, :], bank[2 + k][:, :], ACT.Identity, bias=bqkv_sb[:, n:n + 1]).then_inc(s_qkv_sb, 1)

            def exponentials(c, half):
                sc.wait_ge(s_sub, 2 * c + half + 1)
                sc.activation(prob[:, half, :, :], prob[:, half, :, :], ACT.Exp, scale=SCALE).then_inc(s_exp, 1)

            def banks(half, pattern, **sizes):
                return att_ps[:, 2 * half:2 * half + 2, :].rearrange(pattern, **sizes)

            def prob_t_copy(c, half):
                sc.wait_ge(s_pt, 2 * c + half + 1)
                wait_from_first(sc, s_pv, 2 * (c - 1) + half + 1)
                at = prob_t_at[half]
                sc.activation(prob_t[:, at:at + G * H // 2].rearrange("p (r h w) -> p r w h", h=H, w=2),
                              banks(half, "p a (r w h x) -> p (a r) w h x", w=2, h=H, x=2)[:, :, :, :, half],
                              ACT.Identity).then_inc(s_pt_sb, 1)

            def y_out(c, batch, part, half):
                sc.wait_ge(s_ot, 2 * c + half + 1)
                row = y_t[:, :, bass.ds(batch, 1), :, bass.ds(part * 32 + 16 * half, 16)]
                sc.activation(row.rearrange("p w b h r -> p w (b h) r"),
                              banks(half, "p a (r w h x) -> p w h (a r) x", w=2, h=H, x=2)[:, :, :, :, half],
                              ACT.Identity).then_inc(s_y, 1)

            def act_step(c, cp, front, proj, attend):
                if proj:
                    xT_copy(c - 1, 1 - cp, 1)
                if front:
                    h_copy(c, 0)
                if proj:
                    bias_add(c - 1, 0)
                if front:
                    root(c, 0)
                if proj:
                    bias_add(c - 1, 1)
                if attend:
                    exponentials(c - 2, 0)
                if front:
                    xT_copy(c, cp, 0)
                    h_copy(c, 1)
                if attend:
                    exponentials(c - 2, 1)
                if proj:
                    bias_add(c - 1, 2)
                if front:
                    root(c, 1)
                for half in range(2):
                    if attend:
                        prob_t_copy(c - 2, half)
                if proj:
                    bias_add(c - 1, 3)
                    bias_add(c - 1, 4)
                for half in range(2):
                    if attend:
                        y_out(c - 2, (c - 2) // (NC // NB), (c - 2) % (NC // NB), half)
                if proj:
                    bias_add(c - 1, 5)

            embed_chunks(sc, act_step)

            def root2(p):
                sc.wait_ge(t_mv, 2 * p + 2)
                sc.activation(std[:, :], mean_var[:, :, 1], ACT.Sqrt, bias=eps[:, :]).then_inc(t_std, 1)

            def xn2T_copy(p, k):
                sc.wait_ge(t_xT, p + 1)
                wait_from_first(sc, t_lg, p)
                sc.activation(xn2T[:, :, :], bank[k][:, :].rearrange("p (h t) -> p h t", h=NH2), ACT.Identity
                              ).then_inc(t_xT_sb, 1)

            def logits_out(p, k, b, pp):
                sc.wait_ge(t_lg, p + 1)
                sc.activation(logits[64 * b:64 * b + NX, bass.ds(pp * 2 * P, 2 * P)], att_ps[64 * b:64 * b + NX, k, 0:2 * P],
                              ACT.Identity).then_inc(t_lg_sb, 1)

            HP = QT // 2
            sc.wait_ge(c_fill, 1)
            root2(0)
            for k in range(2):
                root2(k + 1)
                xn2T_copy(k, k)
                logits_out(k, k, 0, k)
            with sc.Fori(1, HP // 2) as i:
                for k in range(2):
                    root2(2 * i + k + 1)
                    xn2T_copy(2 * i + k, k)
                    logits_out(2 * i + k, k, 0, 2 * i + k)
            with sc.Fori(HP // 2, HP - 1) as i:
                for k in range(2):
                    root2(2 * i + k + 1)
                    xn2T_copy(2 * i + k, k)
                    logits_out(2 * i + k, k, 1, 2 * i + k - HP)
            for k in range(2):
                p = NT // 2 - 2 + k
                if k == 0:
                    root2(p + 1)
                xn2T_copy(p, k)
                logits_out(p, k, 1, p - HP)

            sc.wait_ge(c_dve, 8)
            sc.activation(sel_w[:, :], sel_v[:, :], ACT.Exp).then_inc(c_exp, 1)

            sc.wait_ge(c_done, 2)
            h_bank = [att_ps[:, n, :] for n in range(4)]

            sc.wait_ge(s_b1, 16)
            def gelus(e, k):
                for half in range(2):
                    sc.wait_ge(e_h, 2 * e + half + 1)
                    if half == 0:
                        wait_from_first(sc, e_y, e - 1)
                    for q in range(4):
                        n = 4 * half + q
                        last = sc.activation(act[:, k, n, :], h_bank[2 * k + half][:, q * P:(q + 1) * P], ACT.Gelu,
                                             bias=b1_sb[:, bass.ds(e * SUB * MH + n, 1)])
                    last.then_inc(e_act, 1)

            for e in range(2):
                gelus(e, e)
            with sc.Fori(1, NX // 2) as i:
                for k in range(2):
                    gelus(2 * i + k, k)

        @block.vector
        def _(dve):
            dve.memset(prob_t[:, G * H // 2:G * H // 2 + 1], 0.0).then_inc(s_zero, 1)
            dve.memset(b_sb[:, :], 0.0).then_inc(s_bzero, 1)
            for n in range(2):
                dve.memset(k_bd[n][:, :, :], 0.0).then_inc(s_zero, 1)

            def rowsT_copy(c, j):
                dve.wait_ge(s_rowsT, 2 * c + j + 1)
                wait_from_first(dve, s_h, 2 * c + j)
                dve.tensor_copy(rowsT[:, :], bank[0][:, 0:P]).then_inc(s_rowsT_sb, 1)

            def norm(src, dst, p, m_bn, m_mv, m_std, m_rstd, m_out):
                for k in range(2):
                    dve.bn_stats(bn6[:, k, :], src[:, k, :]).then_inc(m_bn, 1)
                dve.wait_ge(m_bn, 2 * p + 2)
                dve.memset(pad[:, 0:1], 0.0)
                for k in range(2):
                    dve.bn_aggr(mean_var[:, k, :], bn6[:, k, :]).then_inc(m_mv, 1)
                dve.wait_ge(m_std, p + 1)
                dve.reciprocal(rstd[:, :], std[:, :]).then_inc(m_rstd, 1)
                dve.wait_ge(m_rstd, p + 1)
                for k in range(2):
                    last = dve.tensor_scalar(dst[:, k, :], src[:, k, :], mean_var[:, k, 0:1], rstd[:, k:k + 1],
                                             ALU.subtract, ALU.mult)
                last.then_inc(m_out, 1)

            def pair_norm(c, j):
                dve.wait_ge(s_h_sb, 2 * c + j + 1)
                wait_from_first(dve, s_xT, 2 * c + j)
                norm(h_sb, xn, 2 * c + j, s_bn, s_mv, s_std, s_rstd, s_xn)

            def half_of_banks(half):
                return att_ps[:, 2 * half:2 * half + 2, :].rearrange("p a (x h) -> p (a x) h", h=H)

            def across(v, half):
                return v[:, half, :].unsqueeze(2).to_broadcast([P, NR, H])

            def less_max(c, half):
                n = 2 * c + half
                dve.wait_ge(s_sc, n + 1)
                dve.tensor_reduce(row_max[:, half, :], half_of_banks(half), axis=AX.X, op=ALU.max).then_inc(s_max, 1)
                dve.wait_ge(s_max, n + 1)
                wait_from_first(dve, s_ot, n - 1)
                dve.tensor_tensor(prob[:, half, :, :], half_of_banks(half), across(row_max, half),
                                  ALU.subtract).then_inc(s_sub, 1)

            def sums(c, half):
                n = 2 * c + half
                dve.wait_ge(s_exp, n + 1)
                dve.tensor_reduce(row_sum[:, half, :], prob[:, half, :, :], axis=AX.X, op=ALU.add).then_inc(s_sum, 1)
                dve.wait_ge(s_sum, n + 1)
                dve.reciprocal(row_sum[:, half, :], row_sum[:, half, :]).then_inc(s_rsum, 1)

            def over_sum(c, half):
                n = 2 * c + half
                dve.wait_ge(s_rsum, n + 1)
                dve.wait_ge(s_pv, n + 1)
                dve.tensor_tensor(prob[:, half, :, :], half_of_banks(half), across(row_sum, half), ALU.mult).then_inc(s_o, 1)

            def dve_step(c, cp, front, proj, attend):
                if front:
                    rowsT_copy(c, 0)
                    pair_norm(c, 0)
                if attend:
                    less_max(c - 2, 0)
                    less_max(c - 2, 1)
                if front:
                    rowsT_copy(c, 1)
                if attend:
                    sums(c - 2, 0)
                    sums(c - 2, 1)
                if front:
                    pair_norm(c, 1)
                if attend:
                    over_sum(c - 2, 0)
                    over_sum(c - 2, 1)

            embed_chunks(dve, dve_step)

            dve.wait_ge(s_y, 2 * NC)
            dve.wait_ge(s_h_st, 32 * NT // 2)
            dve.memset(logits[0:64, :], LOWEST).then_inc(c_fill, 1)

            def out_pair(p, k):
                dve.wait_ge(t_o, p + 1)
                dve.wait_ge(t_res_b, p + 1)
                if not (isinstance(p, int) and p < 2):
                    dve.wait_ge(t_h2_st[k], 16 * ((p - k) // 2))
                dve.tensor_tensor(h2_sb[:, k, :, :], bank[2 + k][:, :].rearrange("p (n e) -> p n e", n=2),
                                  res_sb[:, k, :, :], ALU.add).then_inc(t_h2, 1)
                dve.wait_ge(t_h2, p + 1)
                if not (isinstance(p, int) and p < 2):
                    dve.wait_ge(t_xn_st[k], 16 * ((p - k) // 2))
                wait_from_first(dve, t_xT, p - 1)
                norm(h2_sb[:, k, :, :], xn2[:, k, :, :], p, t_bn, t_mv, t_std, t_rstd, t_xn)

            for k in range(2):
                out_pair(k, k)
            with dve.Fori(1, NT // 4) as i:
                for k in range(2):
                    out_pair(2 * i + k, k)

            dve.wait_ge(t_lg_sb, NT // 2)
            dve.wait_ge(t_att, NT // 2)
            steps = CAP // 8
            top_u = top_at[:, :].bitcast(U32)
            chain = [0]

            def link(ins):
                chain[0] += 1
                ins.then_inc(c_dve, 1)
                dve.wait_ge(c_dve, chain[0])

            c_max = ctx.enter_context(nc.semaphore("c_max"))
            c_rep = ctx.enter_context(nc.semaphore("c_rep"))
            for n in range(steps):
                eight = top[0:LP, 8 * n:8 * n + 8]
                dve.max(eight, logits[0:LP, :]).then_inc(c_max, 1)
                dve.wait_ge(c_max, n + 1)
                dve.max_index(top_u[0:LP, 8 * n:8 * n + 8], eight, logits[0:LP, :]).then_inc(c_rep, 1)
                dve.match_replace(logits[0:LP, :], eight, logits[0:LP, :], LOWEST).then_inc(c_rep, 1)
                dve.wait_ge(c_rep, 2 * n + 2)
            dve.tensor_copy(top_atf[0:LP, :], top_u[0:LP, :]).then_inc(c_top, 1)
            dve.wait_ge(c_top, 1)
            dve.tensor_scalar(top_atf[64:LP, :], top_atf[64:LP, :], float(S), None, ALU.add).then_inc(c_top, 1)
            dve.wait_ge(c_T, 2)
            dve.tensor_copy(topT[:, 0:LP], bank[0][:, 0:LP]).then_inc(c_T_sb, 1)
            dve.tensor_copy(topiT[:, 0:LP], bank[1][:, 0:LP]).then_inc(c_T_sb, 1)
            dve.wait_ge(c_rev, 1)
            dve.wait_ge(c_T_sb, 2)
            link(dve.tensor_tensor(sel_mask[:, :], bank[2][:, 0:NX], topT[:, 0:NX], ALU.is_le))
            link(dve.tensor_tensor(sel_v[:, :], bank[2][:, 0:NX], topT[:, 0:NX], ALU.max))
            link(dve.tensor_copy(sel_max[:, :], bank[2][:, 128:128 + NX]))
            link(dve.tensor_tensor(sel_max[:, :], sel_max[:, :], bank[2][:, 192:192 + NX], ALU.max))
            link(dve.tensor_copy(rev_if[:, :], bank[2][:, 64:64 + NX]))
            link(dve.tensor_tensor(sel_if[:, :], topiT[:, 0:NX], rev_if[:, :], ALU.subtract))
            link(dve.tensor_tensor(sel_if[:, :], sel_if[:, :], sel_mask[:, :], ALU.mult))
            link(dve.tensor_tensor(sel_v[:, :], sel_v[:, :], sel_max[:, :], ALU.subtract))
            dve.tensor_tensor(tok_idx[:, :], sel_if[:, :], rev_if[:, :], ALU.add).then_inc(c_done, 1)
            dve.wait_ge(c_sum, 1)
            link(dve.reciprocal(sel_rden[:, :], bank[3][:, 0:NX]))
            dve.tensor_tensor(sel_w[:, :], sel_w[:, :], sel_rden[:, :], ALU.mult).then_inc(c_done, 1)
            dve.wait_ge(c_done, 2)

            def xgT_copy(e, k):
                dve.wait_ge(e_xgT, e + 1)
                wait_from_first(dve, e_h, 2 * (e - 1))
                dve.tensor_copy(xgT[:, k, :], bank[k][:, 0:E]).then_inc(e_xgT_sb, 1)

            def y_out(e, k, s, use):
                dve.wait_ge(e_y, e + 1)
                if not (isinstance(e, int) and e < 4):
                    dve.wait_ge(e_out, 16 * (e - 3))
                dve.wait_ge(e_b2[s], 16 * use)
                dve.tensor_tensor(y_sb[:, s, :], bank[2 + k][:, 0:E], b2_sb[:, s, :], ALU.add).then_inc(e_yb, 1)
                dve.wait_ge(e_yb, e + 1)
                dve.tensor_scalar(y_sb[:, s, :], y_sb[:, s, :], sel_w[:, bass.ds(e, 1)], None,
                                  ALU.mult).then_inc(e_y_sb, 1)

            xgT_copy(0, 0)
            for e in range(1, 4):
                xgT_copy(e, e % 2)
                y_out(e - 1, (e - 1) % 2, e - 1, 1)
            with dve.Fori(1, NX // 4) as i:
                for s in range(4):
                    e = 4 * i + s
                    xgT_copy(e, s % 2)
                    y_out(e - 1, (s + 1) % 2, (s + 3) % 4, i + (s > 0))
            y_out(NX - 1, 1, 3, NX // 4)


def kernel(x, L0_tok_A, L0_tok_B, L0_attn_Wq, L0_attn_bq, L0_attn_Wk, L0_attn_bk, L0_attn_Wv, L0_attn_bv,
           L0_attn_Wo, L0_attn_bo, L0_ffn_Wr, L0_ffn_W1, L0_ffn_b1, L0_ffn_W2, L0_ffn_b2):
    import numpy as np
    import concourse.bacc as bacc
    from concourse.bass_utils import run_bass_kernel_spmd

    P_ = 128
    c = np.ascontiguousarray
    x, A, B = np.asarray(x), np.asarray(L0_tok_A), np.asarray(L0_tok_B)
    E = B.shape[1]
    W1, W2 = np.asarray(L0_ffn_W1), np.asarray(L0_ffn_W2)
    NX, SUB, _, MID = W1.shape
    K = W2.shape[3]
    arrays = {
        "ids": c(x.reshape(-1, 64, 4, 2).transpose(3, 1, 0, 2)).reshape(P_, -1),
        "A": c(A), "B": c(B),
        "WqT": c(np.asarray(L0_attn_Wq).T), "WkT": c(np.asarray(L0_attn_Wk).T),
        "WvT": c(np.asarray(L0_attn_Wv).T), "WoT": c(np.asarray(L0_attn_Wo).T),
        "bqkv": c(np.concatenate([np.asarray(v).reshape(-1, P_) for v in (L0_attn_bq, L0_attn_bk, L0_attn_bv)]).T),
        "bo": c(np.asarray(L0_attn_bo).reshape(1, E)),
        "WrT": c(np.asarray(L0_ffn_Wr).T),
        "W1": c(W1.reshape(NX, SUB, E // P_, P_, MID).transpose(0, 3, 2, 1, 4)).reshape(NX, P_, -1),
        "b1T": c(np.asarray(L0_ffn_b1).reshape(-1, P_).T),
        "W2": c(W2.reshape(NX, SUB, MID // P_, P_, K).transpose(0, 3, 1, 2, 4)).reshape(NX, P_, -1),
        "b2": c(np.asarray(L0_ffn_b2).reshape(NX, E)),
    }
    nc = bacc.Bacc("TRN2", target_bir_lowering=False, num_devices=1)
    args = [nc.dram_tensor(n, a.shape, mybir.dt.from_np(a.dtype), kind="ExternalInput").ap() for n, a in arrays.items()]
    args.append(nc.dram_tensor("out", (x.size, E), F32, kind="ExternalOutput").ap())
    tower_kernel(nc, *args)
    r = run_bass_kernel_spmd(nc, [arrays], core_ids=[0])
    return r.results[0]["out"].reshape(*x.shape, E)
```

```python
from contextlib import ExitStack

import concourse.bass as bass
from concourse import mybir

P = 128
F32 = mybir.dt.float32
BF16 = mybir.dt.bfloat16
I32 = mybir.dt.int32
U32 = mybir.dt.uint32
ALU = mybir.AluOpType
ACT = mybir.ActivationFunctionType
AX = mybir.AxisListType
LN_EPS = 1e-5
LOWEST = -3.0e38


def wait_from_first(eng, sem, count):
    if isinstance(count, int) and count <= 0:
        return
    eng.wait_ge(sem, count)


def tower_kernel(nc, ids, A, B, WqT, WkT, WvT, WoT, bqkv, bo, WrT, W1, b1T, W2, b2T, out):
    RANK, E = B.shape
    NX, _, EW = W1.shape
    T = ids.shape[0] * ids.shape[1]
    NB, S = 2, T // 2
    NT = T // P
    H, D = 16, E // 16
    NH2 = E // P
    CH = 512
    TC = CH // P
    NC = T // CH

    SUB = 4
    MID = EW // (NH2 * SUB)
    MH = MID // P
    KO = E // SUB
    CAP = int(1.5 * T / NX)
    FIRST = 80
    SCALE = 1.0 / float(D) ** 0.5
    G = CH // 8
    assert CAP == P and NB * NX <= P and NC % 2 == 0 and G == 64 and 8 * D == P and H == D

    h_dram = nc.dram_tensor("h_dram", [T, E], F32).ap()
    qkv_dram = nc.dram_tensor("qkv_dram", [NC, 3, E, CH], F32).ap()
    xn_dram = nc.dram_tensor("xn_dram", [T, E], F32).ap()

    ctx = ExitStack()
    with ctx:
        def sb(name, shape, dt=F32):
            return ctx.enter_context(nc.sbuf_tensor(name, shape, dt))

        def sem(name):
            return ctx.enter_context(nc.semaphore(name))

        big = sb("big", [P, 4 * P * G])
        k_bd = [big[:, n * P * G:(n + 1) * P * G].rearrange("p (m g) -> p m g", g=G) for n in (0, 1)]
        v_bd = [big[:, n * P * G:(n + 1) * P * G].rearrange("p (m g) -> p m g", g=G) for n in (2, 3)]
        WN = EW + SUB * MH * KO
        WS = 12
        w_slot = [big[:, s * WN:(s + 1) * WN] for s in range(WS)]
        q_op = sb("q_op", [P, H, G])
        y_t = sb("y_t", [P, NH2, NB, H, P])
        work = sb("work", [P, 5760])
        ident = sb("ident", [P, P])
        eps = sb("eps", [P, 1])
        pad = sb("pad", [P, 2])
        ids_sb = sb("ids_sb", [P, NT], I32)
        b_sb = sb("b_sb", [P, 2 * E])
        bqkv_sb = sb("bqkv_sb", [P, 3 * NH2])
        wo_sb = sb("wo_sb", [P, NH2, E])
        wr_sb = sb("wr_sb", [P, NH2, NX])
        bn6 = sb("bn6", [P, 2, 6])
        mean_var = sb("mean_var", [P, 2, 2, 2])
        std = sb("std", [P, 2, 2])
        rstd = sb("rstd", [P, 2])
        rows_sb = sb("rows_sb", [P, 2 * TC, RANK])

        def carve(base, at, n):
            return base[:, at:at + n], at + n

        at = 0
        wqkv_sb, at = carve(work, at, 3 * NH2 * E)
        wqkv_sb = wqkv_sb.rearrange("p (w h e) -> p w h e", w=3, h=NH2)
        xnT, at = carve(work, at, 2 * NH2 * CH)
        xnT = xnT.rearrange("p (k h t) -> p k h t", k=2, h=NH2)
        rowsT, at = carve(work, at, P)
        h_sb, at = carve(work, at, 2 * E)
        h_sb = h_sb.rearrange("p (k e) -> p k e", k=2)
        xn, at = carve(work, at, 2 * E)
        xn = xn.rearrange("p (k e) -> p k e", k=2)
        NR = G // 8 * 8
        prob = sb("prob", [P, 2, NR, H])
        prob_t = sb("prob_t", [P, G * H + 1])
        prob_t_at = (0, G * H // 2 + 1)
        row_max = sb("row_max", [P, 2, NR])
        row_sum = sb("row_sum", [P, 2, NR])
        qkv_sb, at = carve(work, at, 2 * CH)
        qkv_sb = qkv_sb.rearrange("p (k t) -> p k t", k=2)
        assert at <= 5760
        at = 0
        res_sb, at = carve(work, at, 4 * E)
        h2_sb, at = carve(work, at, 4 * E)
        xn2, at = carve(work, at, 4 * E)
        res_sb, h2_sb, xn2 = (v.rearrange("p (k n e) -> p k n e", k=2, n=2) for v in (res_sb, h2_sb, xn2))
        prob_f = prob[:, :, :, :].rearrange("p a g h -> p (a g h)")
        xn2T = prob_f[:, 4 * E:8 * E].rearrange("p (k h t) -> p k h t", k=2, h=NH2)
        bo_sb, _ = carve(b_sb, 0, E)
        logits, at = carve(work, at, S)
        LP = 64 + NX
        att0, at = carve(work, at, 2 * E)
        att_sb = [v.rearrange("p (h n r) -> p h n r", h=NH2, n=2)
                  for v in (att0, rows_sb[:, :, :].rearrange("p k r -> p (k r)"))]
        assert at <= 5760
        y_flat = y_t[:, :, :, :, :].rearrange("p w b h r -> p (w b h r)")
        at = 0
        top, at = carve(y_flat, at, CAP)
        top_at, at = carve(y_flat, at, CAP)
        top_atf, at = carve(y_flat, at, CAP)
        top_hi, at = carve(y_flat, at, CAP)
        top_hi = top_hi.bitcast(U32)
        top_hif, at = carve(y_flat, at, CAP)
        topT, at = carve(y_flat, at, P)
        topiT, at = carve(y_flat, at, P)
        b2_sb, at = carve(y_flat, at, NX * NH2)
        b1_sb, at = carve(y_flat, at, NX * SUB * MH)
        flip, at = carve(y_flat, at, P)
        first_row, at = carve(y_flat, at, P)
        other, at = carve(y_flat, at, P)
        missed, at = carve(y_flat, at, 3)
        SEG = 32
        cand, at = carve(y_flat, at, S // SEG * 8)
        seg_low, at = carve(y_flat, at, 1)
        tie, at = carve(y_flat, at, FIRST // 8 - 1)
        missed_n, at = carve(y_flat, at, 1)
        missed_n = missed_n.bitcast(I32)
        ones, at = carve(y_flat, at, P)
        sel_mask, at = carve(y_flat, at, NX)
        sel_v, at = carve(y_flat, at, NX)
        sel_max, at = carve(y_flat, at, NX)
        sel_w, at = carve(y_flat, at, NX)
        sel_if, at = carve(y_flat, at, NX)
        sel_rden, at = carve(y_flat, at, NX)
        rev_if, at = carve(y_flat, at, NX)
        tok_idx, at = carve(y_flat, at, NX)
        tok_idx = tok_idx.bitcast(I32)
        at = 0
        xg, at = carve(work, at, 4 * E)
        xg = xg.rearrange("p (k e) -> p k e", k=4)
        xgT, at = carve(work, at, 2 * E)
        xgT = xgT.rearrange("p (k e) -> p k e", k=2)
        act, at = carve(work, at, 2 * SUB * MH * P)
        act = act.rearrange("p (k s t) -> p k s t", k=2, t=P)
        yT_sb, at = carve(work, at, E)
        y_sb, at = carve(work, at, 4 * E)
        y_sb = y_sb.rearrange("p (k e) -> p k e", k=4)
        assert at <= 5760

        bank = [ctx.enter_context(nc.psum_tensor(f"bank{i}", [P, CH], F32)) for i in range(4)]
        att_ps = ctx.enter_context(nc.psum_tensor("att_ps", [P, 4, CH], F32))

        s_const = sem("s_const")
        s_id = sem("s_id")
        s_other = sem("s_other")
        s_zero = sem("s_zero")
        s_zero1 = sem("s_zero1")
        s_bzero = sem("s_bzero")
        s_ids = sem("s_ids")
        s_w = sem("s_w")
        s_rows = [sem(f"s_rows{k}") for k in range(8)]
        s_rowsT = sem("s_rowsT")
        s_rowsT_sb = sem("s_rowsT_sb")
        s_h = sem("s_h")
        s_h_sb = sem("s_h_sb")
        s_h_st0 = sem("s_h_st0")
        s_h_st = sem("s_h_st")
        s_bn = sem("s_bn")
        s_mv = sem("s_mv")
        s_std = sem("s_std")
        s_rstd = sem("s_rstd")
        s_xn = sem("s_xn")
        s_xT = sem("s_xT")
        s_xT_sb = sem("s_xT_sb")
        s_qkv = sem("s_qkv")
        s_qkv_sb = sem("s_qkv_sb")
        s_qkv_st = [sem(f"s_qkv_st{n}") for n in range(6)]
        s_qk = [sem(f"s_qk{k}") for k in range(2)]
        s_v = [sem(f"s_v{k}") for k in range(2)]
        s_sc = sem("s_sc")
        s_max = sem("s_max")
        s_sub = sem("s_sub")
        s_exp = sem("s_exp")
        s_sum = sem("s_sum")
        s_rsum = sem("s_rsum")
        s_pt = sem("s_pt")
        s_pt_sb = sem("s_pt_sb")
        s_pv = sem("s_pv")
        s_o = sem("s_o")
        s_ot = sem("s_ot")
        s_y = sem("s_y")
        s_bo = sem("s_bo")
        t_att = sem("t_att")
        t_res = [sem(f"t_res{k}") for k in range(2)]
        t_res_b = sem("t_res_b")
        t_o = sem("t_o")
        t_h2 = sem("t_h2")
        t_h2_st = [sem(f"t_h2_st{k}") for k in range(2)]
        t_bn = sem("t_bn")
        t_mv = sem("t_mv")
        t_std = sem("t_std")
        t_rstd = sem("t_rstd")
        t_xn = sem("t_xn")
        t_xn_st = [sem(f"t_xn_st{k}") for k in range(2)]
        t_xT = sem("t_xT")
        t_xT_sb = sem("t_xT_sb")
        t_lg = sem("t_lg")
        t_lg_sb = sem("t_lg_sb")
        s_b1 = sem("s_b1")
        s_b2 = sem("s_b2")
        c_pad = sem("c_pad")
        c_cand = sem("c_cand")
        c_low = sem("c_low")
        c_max = sem("c_max")
        c_rep = sem("c_rep")
        c_pos = sem("c_pos")
        c_tie = sem("c_tie")
        s_missed = sem("s_missed")
        c_all_max = sem("c_all_max")
        c_all_rep = sem("c_all_rep")
        c_missed_n = sem("c_missed_n")
        c_fill = sem("c_fill")
        c_top = sem("c_top")
        c_T = sem("c_T")
        c_T_sb = sem("c_T_sb")
        c_rev = sem("c_rev")
        c_dve = sem("c_dve")
        c_exp = sem("c_exp")
        c_sum = sem("c_sum")
        c_done = sem("c_done")
        c_first = sem("c_first")
        c_other = sem("c_other")
        c_miss = sem("c_miss")
        e_w_first = sem("e_w_first")
        e_w = [sem(f"e_w{k}") for k in range(WS)]
        e_xg = [sem(f"e_xg{k}") for k in range(4)]
        e_xgT = sem("e_xgT")
        e_xgT_sb = sem("e_xgT_sb")
        e_h = sem("e_h")
        e_act = sem("e_act")
        e_yT = sem("e_yT")
        e_yT_sb = sem("e_yT_sb")
        e_y = sem("e_y")
        e_y_sb = sem("e_y_sb")
        e_out = sem("e_out")

        block = ctx.enter_context(nc.Block())

        h_rows = h_dram.rearrange("(c g u) e -> c g u e", g=G, u=8)

        def store_h(eng, c, j):
            eng.wait_ge(s_h_sb, 2 * c + j + 1)
            for v in range(2):
                eng.dma_start(h_rows[c, :, 4 * j + v:4 * j + 4:2, :], h_sb[G * v:G * v + G, :, :]).then_inc(
                    s_h_st0 if c == 0 else s_h_st, 16)

        def load_weights(eng, e, slot, done):
            eng.dma_start(slot[:, 0:EW], W1[bass.ds(e, 1), :, :].rearrange("a p n -> (a p) n")).then_inc(done, 16)
            eng.dma_start(slot[:, EW:WN], W2[bass.ds(e, 1), :, :].rearrange("a p n -> (a p) n")).then_inc(done, 16)

        def is_last(c):
            return isinstance(c, int) and c == NC + 1

        def embed_chunks(eng, step):
            step(0, 0, True, False, False)
            step(1, 1, True, True, False)
            step(2, 0, True, True, False)
            step(2, 0, False, False, True)
            step(3, 1, True, True, True)
            with eng.Fori(2, NC // 2) as i:
                for u in range(2):
                    step(2 * i + u, u, True, True, True)
            step(NC, 0, False, True, True)
            step(NC + 1, 1, False, False, True)

        @block.sync
        def _(sp):
            sp.dma_start(ids_sb[:, :], ids).then_inc(s_ids, 16)
            sp.wait_ge(s_bzero, 1)
            for k in range(2):
                sp.dma_start(b_sb[k * RANK:(k + 1) * RANK, k * E:(k + 1) * E], B).then_inc(s_w, 16)
            for n, w in enumerate((WqT, WkT, WvT)):
                sp.dma_start(wqkv_sb[:, n, :, :], w.rearrange("(h p) e -> p h e", p=P)).then_inc(s_w, 16)
            sp.dma_start(bqkv_sb[:, :], bqkv).then_inc(s_w, 16)
            sp.dma_start(wo_sb[:, :, :], WoT.rearrange("(h p) e -> p h e", p=P)).then_inc(s_w, 16)
            sp.dma_start(wr_sb[:, :, :], WrT.rearrange("(h p) e -> p h e", p=P)).then_inc(s_w, 16)

            def operand_source(c, w, t):
                return qkv_dram[bass.ds(c, 1), w, :, G * t:G * t + G]

            def load_k(c, cp):
                sp.wait_ge(s_qkv_st[2], 16 * (c + 1))
                sp.wait_ge(s_qkv_st[3], 16 * (c + 1))
                for u in range(8):
                    if u == 7:
                        wait_from_first(sp, s_sc, 2 * c)
                    sp.dma_start(k_bd[cp][D * u:D * u + D, H * u:H * u + H, :],
                                 operand_source(c, 1, u).rearrange("c (h d) g -> (c d) h g", d=D)).then_inc(s_qk[cp], 16)

            def load_q(c, cp):
                for u in range(8):
                    sp.dma_start(q_op[D * u:D * u + D, :, :],
                                 operand_source(c, 0, u).rearrange("c (h d) g -> (c d) h g", d=D)).then_inc(s_qk[cp], 16)
                    if u == 0:
                        wait_from_first(sp, s_pv, 2 * (c - 1))

            def load_v(c, cp):
                sp.wait_ge(s_qkv_st[4], 16 * (c + 1))
                sp.wait_ge(s_qkv_st[5], 16 * (c + 1))
                for u in range(8):
                    sp.dma_start(v_bd[cp][H * u:H * u + H, D * u:D * u + D, :],
                                 operand_source(c, 2, u).rearrange("c (h d) g -> (c h) d g", d=D)).then_inc(s_v[cp], 16)

            for j in range(2):
                store_h(sp, 0, j)

            def sp_step(c, cp, front, project, attend):
                if isinstance(c, int) and c == 1:
                    sp.wait_ge(s_zero, 3)
                if isinstance(c, int) and c == 2:
                    sp.wait_ge(s_zero1, 5)
                if project:
                    load_k(c - 1, 1 - cp)
                    load_q(c - 1, 1 - cp)
                    load_v(c - 1, 1 - cp)

            embed_chunks(sp, sp_step)

            sp.wait_ge(s_h, NT // 2)
            sp.dma_start(bo_sb[:, :], bo.to_broadcast([P, E])).then_inc(s_bo, 16)
            sp.wait_ge(s_qkv, 6 * NC)
            sp.wait_ge(s_h_st, 32 * (NT // 2 - 2))

            def load_res(p, k):
                wait_from_first(sp, t_res_b, p - 1)
                sp.dma_start(res_sb[:, k, :, :], h_dram[bass.ds(p * 2 * P, 2 * P), :].rearrange("(n p) e -> p n e", p=P)
                             ).then_inc(t_res[k], 16)

            def store_pair(p, k):
                sp.wait_ge(t_h2, p + 1)
                sp.dma_start(out[bass.ds(p * 2 * P, 2 * P), :].rearrange("(n p) e -> p n e", p=P), h2_sb[:, k, :, :]
                             ).then_inc(t_h2_st[k], 16)
                sp.wait_ge(t_xn, p + 1)
                sp.dma_start(xn_dram[bass.ds(p * 2 * P, 2 * P), :].rearrange("(n p) e -> p n e", p=P), xn2[:, k, :, :]
                             ).then_inc(t_xn_st[k], 16)

            load_res(0, 0)
            load_res(1, 1)
            for k in range(2):
                load_res(k + 2, k)
                store_pair(k, k)
            with sp.Fori(1, NT // 4 - 1) as i:
                for k in range(2):
                    load_res(2 * i + k + 2, k)
                    store_pair(2 * i + k, k)
            for k in range(2):
                store_pair(NT // 2 - 2 + k, k)

            sp.wait_ge(t_att, NT // 2)
            sp.dma_start(b1_sb[:, :], b1T).then_inc(s_b1, 16)
            sp.dma_start(b2_sb[:, :], b2T).then_inc(s_b2, 16)
            with sp.Fori(0, WS) as s:
                load_weights(sp, s, big[:, bass.ds(s * WN, WN)], e_w_first)

            with sp.Fori(0, NX // WS - 1) as i:
                for s in range(WS):
                    e = i * WS + s
                    new = sp.snap(e + WS)
                    sp.wait_ge(e_yT, e + 1)
                    load_weights(sp, new, w_slot[s], e_w[s])
            sp.wait_ge(e_out, 16 * NX)

        @block.gpsimd
        def _(pool):
            pool.memset(ident[:, :], 0.0).then_inc(s_id, 1)
            pool.memset(eps[:, :], LN_EPS).then_inc(s_const, 1)
            pool.wait_ge(s_id, 1)
            pool.affine_select(out=ident[:, :], in_=ident[:, :], compare_op=ALU.not_equal, fill=1.0,
                               base=0, pattern=[[-1, P]], channel_multiplier=1).then_inc(s_const, 1)

            def gather(t):
                k = t % (2 * TC)
                if t >= 2 * TC:
                    pool.wait_ge(s_rowsT, (t - 2 * TC) // 2 + 1)
                pool.indirect_dma_start(out=rows_sb[:, k, :], out_offset=None, in_=A,
                                        in_offset=bass.IndirectOffsetOnAxis(ap=ids_sb[:, t:t + 1], axis=0)
                                        ).then_inc(s_rows[k], 16)

            pool.wait_ge(s_ids, 16)
            for t in range(2 * TC):
                gather(t)
            pool.memset(v_bd[0][:, :, :], 0.0).then_inc(s_zero, 1)
            pool.memset(k_bd[1][:, :, :], 0.0).then_inc(s_zero1, 1)

            def store_qkv(c, n):
                pool.wait_ge(s_qkv_sb, 6 * c + n + 1)
                pool.dma_start(qkv_dram[c, n // 2, (n % 2) * P:(n % 2) * P + P, :], qkv_sb[:, n % 2, :]
                               ).then_inc(s_qkv_st[n], 16)

            def store_and_gather(c, j):
                if 0 < c < NC:
                    store_h(pool, c, j)
                if c + 2 < NC:
                    for k in range(2):
                        gather((c + 2) * TC + 2 * j + k)

            for c in range(NC + 1):
                for n in range(6):
                    if c > 0:
                        store_qkv(c - 1, n)
                    if n in (0, 2):
                        store_and_gather(c, n // 2)

            for n in (4, 5):
                pool.wait_ge(s_qkv_st[n], 16 * NC)
            pool.wait_ge(s_h_st, 32 * (NT // 2 - 2))
            pool.wait_ge(s_xT_sb, NT // 2)
            pool.memset(logits[0:64, :], LOWEST).then_inc(c_fill, 1)

            def bias_pair(p, k):
                pool.wait_ge(t_res[k], 16 * ((p - k) // 2 + 1))
                if not (isinstance(p, int) and p < 2):
                    pool.wait_ge(t_xn, p - 1)
                    pool.wait_ge(t_h2_st[k], 16 * ((p - k) // 2))
                pool.tensor_tensor(h2_sb[:, k, :, :], res_sb[:, k, :, :], bo_sb[:, :].unsqueeze(1).to_broadcast([P, 2, E]),
                                   ALU.add).then_inc(t_res_b, 1)

            pool.wait_ge(s_bo, 16)
            for k in range(2):
                bias_pair(k, k)
            with pool.Fori(1, NT // 4) as i:
                for k in range(2):
                    bias_pair(2 * i + k, k)

            pool.wait_ge(t_att, NT // 2)
            pool.memset(flip[:, :], 0.0).then_inc(s_id, 1)
            pool.memset(first_row[:, :], 0.0).then_inc(s_id, 1)
            pool.memset(other[:, :], 0.0).then_inc(s_id, 1)
            pool.memset(missed[:, :], 0.0).then_inc(s_missed, 1)
            pool.memset(ones[:, :], 1.0).then_inc(s_const, 1)
            pool.wait_ge(s_id, 4)
            for n, base in enumerate((-64, 64)):
                pool.affine_select(out=other[:, :], in_=other[:, :], compare_op=ALU.not_equal, fill=1.0,
                                   base=base, pattern=[[-1, P]], channel_multiplier=1).then_inc(s_other, 1)
                pool.wait_ge(s_other, n + 1)
            pool.affine_select(out=flip[:, :], in_=flip[:, :], compare_op=ALU.not_equal, fill=1.0,
                               base=1 - P, pattern=[[1, P]], channel_multiplier=1).then_inc(s_const, 1)
            pool.affine_select(out=first_row[:, :], in_=first_row[:, :], compare_op=ALU.not_equal, fill=1.0,
                               base=0, pattern=[[0, P]], channel_multiplier=1).then_inc(s_const, 1)

            pool.wait_ge(c_done, 1)
            for k in range(2):
                pool.wait_ge(t_xn_st[k], 16 * NT // 4)
                pool.wait_ge(t_h2_st[k], 16 * NT // 4)

            def fetch(e):
                if e >= 4:
                    pool.wait_ge(e_xgT, e - 3)
                pool.indirect_dma_start(out=xg[:, e % 4, :], out_offset=None, in_=xn_dram,
                                        in_offset=bass.IndirectOffsetOnAxis(ap=tok_idx[:, e:e + 1], axis=0)
                                        ).then_inc(e_xg[e % 4], 16)

            def add_out(e):
                pool.wait_ge(e_y_sb, e + 1)
                if e > 0:
                    pool.wait_ge(e_out, 16 * e)
                pool.indirect_dma_start(out=out, out_offset=bass.IndirectOffsetOnAxis(ap=tok_idx[:, e:e + 1], axis=0),
                                        in_=y_sb[:, e % 4, :], in_offset=None, compute_op=ALU.add).then_inc(e_out, 16)

            for e in range(NX + 4):
                if e < NX:
                    fetch(e)
                if e >= 4:
                    add_out(e - 4)

        @block.tensor
        def _(pe):
            pe.wait_ge(s_const, 2)
            pe.wait_ge(s_w, 16 * 8)

            def rows_transpose(c, cp, j):
                slot = cp * TC + 2 * j
                pe.wait_ge(s_rows[slot], 16 * ((c - cp) // 2 + 1))
                pe.wait_ge(s_rows[slot + 1], 16 * ((c - cp) // 2 + 1))
                wait_from_first(pe, s_h_sb, 2 * c + j)
                pe.transpose(bank[0][:, 0:P], rows_sb[:, slot:slot + 2, :].rearrange("p k r -> p (k r)"),
                             ident[:, :]).then_inc(s_rowsT, 1)

            def embed(c, j):
                pe.wait_ge(s_rowsT_sb, 2 * c + j + 1)
                pe.matmul(bank[0][:, :], rowsT[:, :], b_sb[:, :], start=True, stop=True).then_inc(s_h, 1)

            def xn_transpose(c, j):
                pe.wait_ge(s_xn, 2 * c + j + 1)
                wait_from_first(pe, s_xT_sb, 2 * c + j)
                for h in range(NH2):
                    for k in range(2):
                        last = pe.transpose(bank[1][:, (2 * h + k) * P:(2 * h + k + 1) * P],
                                            xn[:, k, h * P:(h + 1) * P], ident[:, :])
                last.then_inc(s_xT, 1)

            def project(c, cp, n):
                if n == 0:
                    pe.wait_ge(s_xT_sb, 2 * c + 2)
                wait_from_first(pe, s_qkv_sb, 6 * c + n - 1)
                f = (n % 2) * P
                for h in range(NH2):
                    last = pe.matmul(bank[2 + n % 2][:, :], wqkv_sb[:, n // 2, h, f:f + P], xnT[:, cp, h, :],
                                     start=(h == 0), stop=(h == NH2 - 1))
                last.then_inc(s_qkv, 1)

            def block(half, b):
                return 2 * half + b // 4, slice((b % 4) * P, (b % 4 + 1) * P)

            def scores(c, cp, half):
                if half == 0:
                    pe.wait_ge(s_qk[cp], 16 * 16 * ((c - cp) // 2 + 1))
                wait_from_first(pe, s_y, 2 * (c - 1) + half + 1)
                q_pairs = q_op[:, :, :].rearrange("p h (a g) -> p (h a) g", a=2)
                for b in range(8):
                    bk, cols = block(half, b)
                    for q in range(4):
                        g = 32 * half + 4 * b + q
                        last = pe.matmul(att_ps[32 * q:32 * q + 32, bk, cols], q_pairs[:, :, g - 32 * half], k_bd[cp][:, :, g],
                                         start=True, stop=True)
                last.then_inc(s_sc, 1)

            def prob_transpose(c, half):
                pe.wait_ge(s_exp, 2 * c + half + 1)
                for b in range(8):
                    bk, cols = block(half, b)
                    last = pe.transpose(att_ps[:, bk, cols], prob_f[:, (8 * half + b) * P:(8 * half + b + 1) * P], ident[:, :])
                last.then_inc(s_pt, 1)

            def value_product(c, cp, half):
                if half == 0:
                    pe.wait_ge(s_v[cp], 16 * 8 * ((c - cp) // 2 + 1))
                pe.wait_ge(s_pt_sb, 2 * c + half + 1)
                for b in range(8):
                    bk, cols = block(half, b)
                    for q in range(4):
                        g = 32 * half + 4 * b + q
                        at = prob_t_at[half] + 32 * ((4 * b + q) // 2) + q % 2 - half
                        last = pe.matmul(att_ps[32 * q:32 * q + 32, bk, cols], prob_t[:, at:at + 32], v_bd[cp][:, :, g],
                                         start=True, stop=True)
                last.then_inc(s_pv, 1)

            def out_transpose(c, half):
                pe.wait_ge(s_o, 2 * c + half + 1)
                for b in range(8):
                    bk, cols = block(half, b)
                    last = pe.transpose(att_ps[:, bk, cols], prob_f[:, (8 * half + b) * P:(8 * half + b + 1) * P], ident[:, :])
                last.then_inc(s_ot, 1)

            def wo_product(p, k):
                pe.wait_ge(t_att, p + 1)
                wait_from_first(pe, t_h2, p - 1)
                for n in range(2):
                    for h in range(NH2):
                        last = pe.matmul(bank[2 + k][:, n * E:(n + 1) * E], att_sb[k][:, h, n, :], wo_sb[:, h, :],
                                         start=(h == 0), stop=(h == NH2 - 1))
                last.then_inc(t_o, 1)

            def pe_step(c, cp, front, proj, attend):
                def proj_half(n):
                    if proj:
                        project(c - 1, 1 - cp, n)

                if front:
                    rows_transpose(c, cp, 0)
                proj_half(0)
                if front:
                    embed(c, 0)
                proj_half(1)
                if attend:
                    scores(c - 2, cp, 0)
                    scores(c - 2, cp, 1)
                if is_last(c):
                    pe.wait_ge(s_qkv_sb, 6 * NC)
                    wo_product(0, 0)
                    wo_product(1, 1)
                if front:
                    rows_transpose(c, cp, 1)
                    xn_transpose(c, 0)
                proj_half(2)
                if front:
                    embed(c, 1)
                if attend:
                    prob_transpose(c - 2, 0)
                proj_half(3)
                if attend:
                    prob_transpose(c - 2, 1)
                    value_product(c - 2, cp, 0)
                proj_half(4)
                if attend:
                    value_product(c - 2, cp, 1)
                if front:
                    xn_transpose(c, 1)
                if attend:
                    out_transpose(c - 2, 0)
                proj_half(5)
                if attend:
                    out_transpose(c - 2, 1)

            embed_chunks(pe, pe_step)

            pe.wait_ge(s_y, 2 * NC)

            def xn2_transpose(p, k):
                pe.wait_ge(t_xn, p + 1)
                wait_from_first(pe, t_xT_sb, p - 1)
                for h in range(NH2):
                    for n in range(2):
                        last = pe.transpose(bank[k][:, (2 * h + n) * P:(2 * h + n + 1) * P],
                                            xn2[:, k, n, h * P:(h + 1) * P], ident[:, :])
                last.then_inc(t_xT, 1)

            def router(p, k):
                pe.wait_ge(t_xT_sb, p + 1)
                wait_from_first(pe, t_lg_sb, p - 1)
                for h in range(NH2):
                    last = pe.matmul(att_ps[64 * k:64 * k + NX, k, 0:2 * P], wr_sb[:, h, :], xn2T[:, k, h, :],
                                     start=(h == 0), stop=(h == NH2 - 1))
                last.then_inc(t_lg, 1)

            xn2_transpose(0, 0)
            wo_product(2, 0)
            xn2_transpose(1, 1)
            router(0, 0)
            wo_product(3, 1)
            with pe.Fori(1, NT // 4 - 1) as i:
                for k in range(2):
                    xn2_transpose(2 * i + k, k)
                    router(2 * i + k - 1, 1 - k)
                    wo_product(2 * i + k + 2, k)
            for k in range(2):
                xn2_transpose(NT // 2 - 2 + k, k)
                router(NT // 2 - 3 + k, 1 - k)
            router(NT // 2 - 1, 1)

            pe.wait_ge(t_lg_sb, NT // 2)
            pe.wait_ge(s_const, 5)
            pe.wait_ge(s_other, 2)
            pe.wait_ge(c_first, 1)
            pe.matmul(bank[2][0:LP, 0:1], other[0:LP, 0:LP], top[0:LP, CAP - FIRST:CAP - FIRST + 1], start=True,
                      stop=True).then_inc(c_other, 1)
            pe.wait_ge(c_miss, 6)
            for n in range(3):
                last = pe.matmul(bank[3][0:1, 0:1], missed[0:LP, n:n + 1], ones[0:LP, 0:1], start=(n == 0), stop=(n == 2))
            last.then_inc(c_other, 1)
            pe.wait_ge(c_top, 5)
            pe.transpose(bank[0][:, 0:LP], top[0:LP, :], ident[0:LP, 0:LP]).then_inc(c_T, 1)
            pe.transpose(bank[1][:, 0:LP], top_atf[0:LP, :], ident[0:LP, 0:LP]).then_inc(c_T, 1)
            pe.wait_ge(c_T_sb, 2)
            pe.matmul(bank[2][:, 0:NX], flip[:, :], topT[:, 64:64 + NX], start=True, stop=True)
            pe.matmul(bank[2][:, 64:64 + NX], flip[:, :], topiT[:, 64:64 + NX], start=True, stop=True).then_inc(c_rev, 1)
            pe.matmul(att_ps[:, 0, 0:NX], first_row[:, :], topT[:, 0:NX], start=True, stop=True)
            pe.matmul(att_ps[:, 0, 64:64 + NX], first_row[:, :], topT[:, 64:64 + NX], start=True,
                      stop=True).then_inc(c_rev, 1)
            pe.wait_ge(c_exp, 1)
            pe.matmul(bank[3][:, 0:NX], ones[:, :], sel_w[:, :], start=True, stop=True).then_inc(c_sum, 1)

            pe.wait_ge(c_done, 2)
            h_bank = [att_ps[:, n, :] for n in range(4)]

            def tokens_transpose(e, k, s):
                pe.wait_ge(e_xg[s], 16 * ((e - s) // 4 + 1))
                wait_from_first(pe, e_xgT_sb, e - 1)
                for h in range(NH2):
                    last = pe.transpose(bank[k][:, h * P:(h + 1) * P], xg[:, s, h * P:(h + 1) * P], ident[:, :])
                last.then_inc(e_xgT, 1)

            def up(e, k, s, half):
                w1 = w_slot[s][:, 0:EW].rearrange("p (h s m) -> p h s m", h=NH2, s=SUB)
                wait_from_first(pe, e_act, 2 * e + half - 3)
                for q in range(4):
                    ss, mh = (4 * half + q) // MH, (4 * half + q) % MH
                    for h in range(NH2):
                        last = pe.matmul(h_bank[2 * k + half][:, q * P:(q + 1) * P], w1[:, h, ss, mh * P:(mh + 1) * P],
                                         xgT[:, k, h * P:(h + 1) * P], start=(h == 0), stop=(h == NH2 - 1))
                last.then_inc(e_h, 1)

            def down(e, k, s):
                w2 = w_slot[s][:, EW:WN].rearrange("p (s m k) -> p s m k", s=SUB, m=MH)
                pe.wait_ge(e_act, 2 * e + 2)
                wait_from_first(pe, e_y_sb, e - 1)
                for h in range(NH2):
                    for mh in range(MH):
                        for v in range(2):
                            ss = 2 * h + v
                            last = pe.matmul(bank[2 + k][KO * v:KO * v + KO, h * P:(h + 1) * P], w2[:, ss, mh, :],
                                             act[:, k, MH * ss + mh, :], start=(mh == 0), stop=(mh == MH - 1))
                last.then_inc(e_yT, 1)

            def turn(e, k):
                pe.wait_ge(e_yT_sb, 2 * e + 2)
                for h in range(NH2):
                    last = pe.transpose(bank[2 + k][:, E + h * P:E + (h + 1) * P], yT_sb[:, h * P:(h + 1) * P], ident[:, :])
                last.then_inc(e_y, 1)

            def expert(e, s, w_use, more=True):
                first = isinstance(e, int)
                if more:
                    tokens_transpose(e + 1, (s + 1) % 2, (s + 1) % 4)
                pe.wait_ge(e_xgT_sb, e + 1)
                if isinstance(w_use, int) and w_use == 0:
                    pe.wait_ge(e_w_first, 32 * WS)
                else:
                    pe.wait_ge(e_w[s], 32 * w_use)
                up(e, s % 2, s, 0)
                if not (first and e < 2):
                    turn(e - 2, s % 2)
                up(e, s % 2, s, 1)
                if not (first and e < 1):
                    down(e - 1, (s + 1) % 2, (s - 1) % WS)

            tokens_transpose(0, 0, 0)
            for e in range(WS):
                expert(e, e, 0)
            with pe.Fori(1, NX // WS - 1) as i:
                for s in range(WS):
                    expert(WS * i + s, s, i)
            for s in range(WS):
                expert(NX - WS + s, s, NX // WS - 1, more=s < WS - 1)
            turn(NX - 2, 0)
            down(NX - 1, 1, WS - 1)
            turn(NX - 1, 1)

        @block.scalar
        def _(sc):
            def h_copy(c, j):
                sc.wait_ge(s_h, 2 * c + j + 1)
                wait_from_first(sc, s_xn, 2 * c + j)
                if isinstance(c, int) and c < 2 and 2 * c + j <= 2:
                    wait_from_first(sc, s_h_st0, 32 * (2 * c + j))
                else:
                    sc.wait_ge(s_h_st, 32 * (2 * c + j - 2))
                sc.activation(h_sb[:, :, :].rearrange("p k e -> p (k e)"), bank[0][:, :], ACT.Identity).then_inc(s_h_sb, 1)

            def root(c, j):
                sc.wait_ge(s_mv, 4 * c + 2 * j + 2)
                sc.activation(std[:, j, :], mean_var[:, j, :, 1], ACT.Sqrt, bias=eps[:, :]).then_inc(s_std, 1)

            def xT_copy(c, cp, j):
                sc.wait_ge(s_xT, 2 * c + j + 1)
                wait_from_first(sc, s_qkv, 6 * (c - 1))
                sc.activation(xnT[:, cp, :, j * 2 * P:(j + 1) * 2 * P], bank[1][:, :].rearrange("p (h t) -> p h t", h=NH2),
                              ACT.Identity).then_inc(s_xT_sb, 1)

            def bias_add(c, n):
                k = n % 2
                sc.wait_ge(s_qkv, 6 * c + n + 1)
                if n >= 2:
                    sc.wait_ge(s_qkv_st[n - 2], 16 * (c + 1))
                else:
                    wait_from_first(sc, s_qkv_st[n + 4], 16 * c)
                sc.activation(qkv_sb[:, k, :], bank[2 + k][:, :], ACT.Identity, bias=bqkv_sb[:, n:n + 1]).then_inc(s_qkv_sb, 1)

            def exponentials(c, half):
                sc.wait_ge(s_sub, 2 * c + half + 1)
                sc.activation(prob[:, half, :, :], prob[:, half, :, :], ACT.Exp, scale=SCALE).then_inc(s_exp, 1)

            def banks(half, pattern, **sizes):
                return att_ps[:, 2 * half:2 * half + 2, :].rearrange(pattern, **sizes)

            def prob_t_copy(c, half):
                sc.wait_ge(s_pt, 2 * c + half + 1)
                wait_from_first(sc, s_pv, 2 * (c - 1) + half + 1)
                at = prob_t_at[half]
                sc.activation(prob_t[:, at:at + G * H // 2].rearrange("p (r h w) -> p r w h", h=H, w=2),
                              banks(half, "p a (r w h x) -> p (a r) w h x", w=2, h=H, x=2)[:, :, :, :, half],
                              ACT.Identity).then_inc(s_pt_sb, 1)

            def y_out(c, batch, part, half):
                sc.wait_ge(s_ot, 2 * c + half + 1)
                row = y_t[:, :, bass.ds(batch, 1), :, bass.ds(part * 32 + 16 * half, 16)]
                sc.activation(row.rearrange("p w b h r -> p w (b h) r"),
                              banks(half, "p a (r w h x) -> p w h (a r) x", w=2, h=H, x=2)[:, :, :, :, half],
                              ACT.Identity).then_inc(s_y, 1)

            def root2(p, k):
                sc.wait_ge(t_mv, 2 * p + 2)
                sc.activation(std[:, k, :], mean_var[:, k, :, 1], ACT.Sqrt, bias=eps[:, :]).then_inc(t_std, 1)

            def lay_pair(p, k):
                wait_from_first(sc, t_o, p - 1)
                HP = H // 2
                sc.activation(att_sb[k].rearrange("p h n r -> p h (n r)"),
                              y_t[:, :, bass.ds(p // HP, 1), bass.ds(2 * (p % HP), 2), :].rearrange("p h b n r -> p h (b n r)"),
                              ACT.Identity).then_inc(t_att, 1)

            def act_step(c, cp, front, proj, attend):
                def bias_half(n):
                    if proj:
                        bias_add(c - 1, n)

                def y_half(half):
                    if attend:
                        y_out(c - 2, (c - 2) // (NC // NB), (c - 2) % (NC // NB), half)

                if is_last(c):
                    for n in (4, 5):
                        sc.wait_ge(s_qkv_st[n], 16 * NC)
                    sc.wait_ge(s_rowsT, NT // 2)
                    lay_pair(0, 0)
                    lay_pair(1, 1)
                bias_half(0)
                if front:
                    h_copy(c, 0)
                bias_half(1)
                if front:
                    root(c, 0)
                if attend:
                    exponentials(c - 2, 0)
                if front:
                    xT_copy(c, cp, 0)
                bias_half(2)
                if front:
                    h_copy(c, 1)
                if attend:
                    exponentials(c - 2, 1)
                    prob_t_copy(c - 2, 0)
                if front:
                    root(c, 1)
                bias_half(3)
                if attend:
                    prob_t_copy(c - 2, 1)
                if is_last(c):
                    root2(0, 0)
                bias_half(4)
                if front:
                    xT_copy(c, cp, 1)
                y_half(0)
                bias_half(5)
                y_half(1)

            embed_chunks(sc, act_step)

            def xn2T_copy(p, k):
                sc.wait_ge(t_xT, p + 1)
                wait_from_first(sc, t_lg, p - 1)
                sc.activation(xn2T[:, k, :, :], bank[k][:, :].rearrange("p (h t) -> p h t", h=NH2), ACT.Identity
                              ).then_inc(t_xT_sb, 1)

            def logits_out(p, k, i):
                sc.wait_ge(t_lg, p + 1)
                sc.activation(logits[64 * k:64 * k + NX, bass.ds(i * 2 * P, 2 * P)], att_ps[64 * k:64 * k + NX, k, 0:2 * P],
                              ACT.Identity).then_inc(t_lg_sb, 1)

            sc.wait_ge(s_y, 2 * NC)
            sc.wait_ge(c_fill, 1)
            for k in range(2):
                lay_pair(k + 2, k)
                root2(k + 1, 1 - k)
                xn2T_copy(k, k)
            logits_out(0, 0, 0)
            with sc.Fori(1, NT // 4 - 1) as i:
                for k in range(2):
                    lay_pair(2 * i + k + 2, k)
                    root2(2 * i + k + 1, 1 - k)
                    xn2T_copy(2 * i + k, k)
                    logits_out(2 * i + k - 1, 1 - k, i - 1 + k)
            for k in range(2):
                p = NT // 2 - 2 + k
                if k == 0:
                    root2(p + 1, 1 - k)
                xn2T_copy(p, k)
                logits_out(p - 1, 1 - k, (p - 1) // 2)
            logits_out(p, k, p // 2)

            sc.wait_ge(c_dve, 12)
            sc.activation(sel_w[:, :], sel_v[:, :], ACT.Exp).then_inc(c_exp, 1)

            sc.wait_ge(c_done, 2)
            h_bank = [att_ps[:, n, :] for n in range(4)]

            sc.wait_ge(s_b1, 16)

            def gelus(e, k):
                for half in range(2):
                    sc.wait_ge(e_h, 2 * e + half + 1)
                    if half == 0:
                        wait_from_first(sc, e_yT, e - 1)
                    for q in range(4):
                        n = 4 * half + q
                        last = sc.activation(act[:, k, n, :], h_bank[2 * k + half][:, q * P:(q + 1) * P], ACT.Gelu,
                                             bias=b1_sb[:, bass.ds(e * SUB * MH + n, 1)])
                    last.then_inc(e_act, 1)

            for e in range(2):
                gelus(e, e)
            with sc.Fori(1, NX // 2) as i:
                for k in range(2):
                    gelus(2 * i + k, k)

        @block.vector
        def _(dve):
            dve.memset(prob_t[:, G * H // 2:G * H // 2 + 1], 0.0).then_inc(s_zero, 1)
            dve.memset(b_sb[:, :], 0.0).then_inc(s_bzero, 1)
            dve.memset(k_bd[0][:, :, :], 0.0).then_inc(s_zero, 1)

            def rowsT_copy(c, j):
                dve.wait_ge(s_rowsT, 2 * c + j + 1)
                wait_from_first(dve, s_h, 2 * c + j)
                dve.tensor_copy(rowsT[:, :], bank[0][:, 0:P]).then_inc(s_rowsT_sb, 1)

            def stats(src, p, k, m_bn, m_mv):
                for n in range(2):
                    dve.bn_stats(bn6[:, n, :], src[:, n, :]).then_inc(m_bn, 1)
                dve.wait_ge(m_bn, 2 * p + 2)
                dve.memset(pad[:, 0:1], 0.0)
                for n in range(2):
                    dve.bn_aggr(mean_var[:, k, n, :], bn6[:, n, :]).then_inc(m_mv, 1)

            def norm(src, dst, p, k, m_std, m_rstd, m_out):
                wait_from_first(dve, m_out, p)
                dve.wait_ge(m_std, p + 1)
                dve.reciprocal(rstd[:, :], std[:, k, :]).then_inc(m_rstd, 1)
                dve.wait_ge(m_rstd, p + 1)
                for n in range(2):
                    last = dve.tensor_scalar(dst[:, n, :], src[:, n, :], mean_var[:, k, n, 0:1], rstd[:, n:n + 1],
                                             ALU.subtract, ALU.mult)
                last.then_inc(m_out, 1)

            def pair_stats(c, j):
                dve.wait_ge(s_h_sb, 2 * c + j + 1)
                stats(h_sb, 2 * c + j, j, s_bn, s_mv)

            def pair_norm(c, j):
                wait_from_first(dve, s_xT, 2 * c + j)
                norm(h_sb, xn, 2 * c + j, j, s_std, s_rstd, s_xn)

            def half_of_banks(half):
                return att_ps[:, 2 * half:2 * half + 2, :].rearrange("p a (x h) -> p (a x) h", h=H)

            def across(v, half):
                return v[:, half, :].unsqueeze(2).to_broadcast([P, NR, H])

            def less_max(c, half):
                n = 2 * c + half
                dve.wait_ge(s_sc, n + 1)
                dve.tensor_reduce(row_max[:, half, :], half_of_banks(half), axis=AX.X, op=ALU.max).then_inc(s_max, 1)
                dve.wait_ge(s_max, n + 1)
                wait_from_first(dve, s_ot, n - 1)
                dve.tensor_tensor(prob[:, half, :, :], half_of_banks(half), across(row_max, half),
                                  ALU.subtract).then_inc(s_sub, 1)

            def sums(c, half):
                n = 2 * c + half
                dve.wait_ge(s_exp, n + 1)
                dve.tensor_reduce(row_sum[:, half, :], prob[:, half, :, :], axis=AX.X, op=ALU.add).then_inc(s_sum, 1)
                dve.wait_ge(s_sum, n + 1)
                dve.reciprocal(row_sum[:, half, :], row_sum[:, half, :]).then_inc(s_rsum, 1)

            def over_sum(c, half):
                n = 2 * c + half
                dve.wait_ge(s_rsum, n + 1)
                dve.wait_ge(s_pv, n + 1)
                dve.tensor_tensor(prob[:, half, :, :], half_of_banks(half), across(row_sum, half), ALU.mult).then_inc(s_o, 1)

            def out_sum(p, k):
                dve.wait_ge(t_o, p + 1)
                dve.wait_ge(t_res_b, p + 1)
                dve.tensor_tensor(h2_sb[:, k, :, :], bank[2 + k][:, :].rearrange("p (n e) -> p n e", n=2),
                                  h2_sb[:, k, :, :], ALU.add).then_inc(t_h2, 1)
                dve.wait_ge(t_h2, p + 1)
                stats(h2_sb[:, k, :, :], p, k, t_bn, t_mv)

            def out_norm(p, k):
                if not (isinstance(p, int) and p < 2):
                    dve.wait_ge(t_xn_st[k], 16 * ((p - k) // 2))
                wait_from_first(dve, t_xT, p - 1)
                norm(h2_sb[:, k, :, :], xn2[:, k, :, :], p, k, t_std, t_rstd, t_xn)

            def dve_step(c, cp, front, proj, attend):
                def zero_v(part):
                    if isinstance(c, int) and c == 1:
                        dve.memset(v_bd[1][:, part * 32:part * 32 + 32, :], 0.0).then_inc(s_zero1, 1)

                if front:
                    rowsT_copy(c, 0)
                    pair_stats(c, 0)
                    pair_norm(c, 0)
                zero_v(0)
                zero_v(1)
                if attend:
                    less_max(c - 2, 0)
                if front:
                    rowsT_copy(c, 1)
                if attend:
                    less_max(c - 2, 1)
                    sums(c - 2, 0)
                if front:
                    pair_stats(c, 1)
                if attend:
                    sums(c - 2, 1)
                if is_last(c):
                    out_sum(0, 0)
                if front:
                    pair_norm(c, 1)
                zero_v(2)
                zero_v(3)
                if attend:
                    over_sum(c - 2, 0)
                if is_last(c):
                    out_norm(0, 0)
                if attend:
                    over_sum(c - 2, 1)

            embed_chunks(dve, dve_step)

            out_sum(1, 1)
            out_norm(1, 1)
            with dve.Fori(1, NT // 4) as i:
                for k in range(2):
                    out_sum(2 * i + k, k)
                    out_norm(2 * i + k, k)

            dve.wait_ge(t_att, NT // 2)
            steps = CAP // 8
            top_u = top_at[:, :].bitcast(U32)
            chain = [0]

            def link(ins):
                chain[0] += 1
                ins.then_inc(c_dve, 1)
                dve.wait_ge(c_dve, chain[0])

            dve.memset(top[:, FIRST:CAP], LOWEST).then_inc(c_pad, 1)
            dve.memset(top_at[:, FIRST:CAP], 0.0).then_inc(c_pad, 1)

            early = S // SEG - 2 * 2 * P // SEG
            dve.wait_ge(t_lg_sb, NT // 2 - 4)
            for n in range(S // SEG):
                if n == early:
                    dve.wait_ge(t_lg_sb, NT // 2)
                last = dve.max(cand[0:LP, 8 * n:8 * n + 8], logits[0:LP, SEG * n:SEG * n + SEG])
            last.then_inc(c_cand, 1)
            dve.wait_ge(c_cand, 1)
            dve.tensor_reduce(seg_low[0:LP, :], cand[0:LP, :].rearrange("p (n k) -> p n k", k=8)[:, :, 7], axis=AX.X,
                              op=ALU.max).then_inc(c_low, 1)
            dve.wait_ge(c_low, 1)
            dve.wait_ge(c_pad, 2)
            for n in range(FIRST // 8):
                eight = top[0:LP, 8 * n:8 * n + 8]
                dve.max(eight, cand[0:LP, :]).then_inc(c_max, 1)
                dve.wait_ge(c_max, n + 1)
                dve.match_replace(cand[0:LP, :], eight, cand[0:LP, :], LOWEST).then_inc(c_rep, 1)
                dve.wait_ge(c_rep, n + 1)
            dve.memset(pad[:, 0:1], 0.0).then_inc(c_first, 1)

            def positions(n):
                return dve.max_index(top_u[0:LP, 8 * n:8 * n + 8], top[0:LP, 8 * n:8 * n + 8], logits[0:LP, :])

            for n in range(3):
                positions(n)
            dve.wait_ge(s_missed, 1)
            eights = top[:, 0:FIRST].rearrange("p (n k) -> p n k", k=8)
            for b in range(NB):
                r = slice(64 * b, 64 * b + NX)
                dve.tensor_tensor(missed[r, 1:2], seg_low[r, :], top[r, FIRST - 1:FIRST], ALU.is_ge).then_inc(c_miss, 1)
                dve.tensor_tensor(tie[r, :], eights[r, 0:FIRST // 8 - 1, 7], eights[r, 1:FIRST // 8, 0], ALU.is_equal
                                  ).then_inc(c_tie, 1)
            dve.wait_ge(c_tie, 2)
            dve.wait_ge(c_other, 1)
            for b in range(NB):
                r = slice(64 * b, 64 * b + NX)
                dve.tensor_reduce(missed[r, 2:3], tie[r, :], axis=AX.X, op=ALU.max).then_inc(c_miss, 1)
                dve.tensor_tensor(missed[r, 0:1], top[r, FIRST - 1:FIRST], bank[2][r, 0:1], ALU.is_ge).then_inc(c_miss, 1)
            for n in range(3, FIRST // 8):
                last = positions(n)
            last.then_inc(c_pos, 1)
            dve.wait_ge(c_other, 2)
            dve.tensor_copy(missed_n[0:1, :], bank[3][0:1, 0:1]).then_inc(c_missed_n, 1)
            dve.wait_ge(c_missed_n, 1)
            dve.wait_ge(c_pos, 1)
            with dve.If(dve.value_load(missed_n[0:1, 0:1]) > 0):
                for n in range(steps):
                    eight = top[0:LP, 8 * n:8 * n + 8]
                    dve.max(eight, logits[0:LP, :]).then_inc(c_all_max, 1)
                    dve.wait_ge(c_all_max, n + 1)
                    dve.max_index(top_u[0:LP, 8 * n:8 * n + 8], eight, logits[0:LP, :]).then_inc(c_all_rep, 1)
                    dve.match_replace(logits[0:LP, :], eight, logits[0:LP, :], LOWEST).then_inc(c_all_rep, 1)
                    dve.wait_ge(c_all_rep, 2 * n + 2)
            dve.tensor_scalar(top_hi[0:LP, :], top_u[0:LP, :], S - 2 * P, None, ALU.bitwise_and).then_inc(c_top, 1)
            dve.tensor_copy(top_atf[0:LP, :], top_u[0:LP, :]).then_inc(c_top, 1)
            dve.wait_ge(c_top, 2)
            dve.tensor_copy(top_hif[0:LP, :], top_hi[0:LP, :]).then_inc(c_top, 1)
            dve.tensor_scalar(top_atf[64:LP, :], top_atf[64:LP, :], float(2 * P), None, ALU.add).then_inc(c_top, 1)
            dve.wait_ge(c_top, 4)
            dve.tensor_tensor(top_atf[0:LP, :], top_atf[0:LP, :], top_hif[0:LP, :], ALU.add).then_inc(c_top, 1)
            dve.wait_ge(c_T, 2)
            dve.tensor_copy(topT[:, 0:LP], bank[0][:, 0:LP]).then_inc(c_T_sb, 1)
            dve.tensor_copy(topiT[:, 0:LP], bank[1][:, 0:LP]).then_inc(c_T_sb, 1)
            dve.wait_ge(c_rev, 1)
            dve.wait_ge(c_T_sb, 2)
            link(dve.tensor_copy(rev_if[:, :], bank[2][:, 64:64 + NX]))
            link(dve.tensor_tensor(sel_max[:, :], bank[2][:, 0:NX], topT[:, 0:NX], ALU.is_equal))
            link(dve.tensor_tensor(sel_mask[:, :], rev_if[:, :], topiT[:, 0:NX], ALU.is_gt))
            link(dve.tensor_tensor(sel_mask[:, :], sel_mask[:, :], sel_max[:, :], ALU.mult))
            link(dve.tensor_tensor(sel_max[:, :], bank[2][:, 0:NX], topT[:, 0:NX], ALU.is_lt))
            link(dve.tensor_tensor(sel_mask[:, :], sel_mask[:, :], sel_max[:, :], ALU.add))
            link(dve.tensor_tensor(sel_if[:, :], topiT[:, 0:NX], rev_if[:, :], ALU.subtract))
            link(dve.tensor_tensor(sel_if[:, :], sel_if[:, :], sel_mask[:, :], ALU.mult))
            dve.tensor_tensor(tok_idx[:, :], sel_if[:, :], rev_if[:, :], ALU.add).then_inc(c_done, 1)
            link(dve.tensor_tensor(sel_v[:, :], bank[2][:, 0:NX], topT[:, 0:NX], ALU.max))
            dve.wait_ge(c_rev, 2)
            link(dve.tensor_copy(sel_max[:, :], att_ps[:, 0, 0:NX]))
            link(dve.tensor_tensor(sel_max[:, :], sel_max[:, :], att_ps[:, 0, 64:64 + NX], ALU.max))
            link(dve.tensor_tensor(sel_v[:, :], sel_v[:, :], sel_max[:, :], ALU.subtract))
            dve.wait_ge(c_sum, 1)
            link(dve.reciprocal(sel_rden[:, :], bank[3][:, 0:NX]))
            dve.tensor_tensor(sel_w[:, :], sel_w[:, :], sel_rden[:, :], ALU.mult).then_inc(c_done, 1)
            dve.wait_ge(c_done, 2)

            def xgT_copy(e, k):
                dve.wait_ge(e_xgT, e + 1)
                wait_from_first(dve, e_h, 2 * (e - 1))
                dve.tensor_copy(xgT[:, k, :], bank[k][:, 0:E]).then_inc(e_xgT_sb, 1)

            def yT_copy(e, k):
                dve.wait_ge(e_yT, e + 1)
                wait_from_first(dve, e_y, e)
                for h in range(NH2):
                    dve.tensor_scalar(yT_sb[:, h * P:(h + 1) * P], bank[2 + k][:, h * P:(h + 1) * P],
                                      b2_sb[:, bass.ds(NH2 * e + h, 1)], None, ALU.add).then_inc(e_yT_sb, 1)

            def y_out(e, k, s):
                dve.wait_ge(e_y, e + 1)
                if not (isinstance(e, int) and e < 4):
                    dve.wait_ge(e_out, 16 * (e - 3))
                dve.tensor_scalar(y_sb[:, s, :], bank[2 + k][:, E:2 * E], sel_w[:, bass.ds(e, 1)], None,
                                  ALU.mult).then_inc(e_y_sb, 1)

            dve.wait_ge(s_b2, 16)
            xgT_copy(0, 0)
            for e in range(8):
                if e >= 2:
                    yT_copy(e - 2, e % 2)
                xgT_copy(e + 1, (e + 1) % 2)
                if e >= 2:
                    y_out(e - 2, e % 2, (e + 2) % 4)
            with dve.Fori(2, NX // 4 - 1) as i:
                for s in range(4):
                    e = 4 * i + s
                    yT_copy(e - 2, s % 2)
                    xgT_copy(e + 1, (s + 1) % 2)
                    y_out(e - 2, s % 2, (s + 2) % 4)
            for e in range(NX - 4, NX + 2):
                yT_copy(e - 2, e % 2)
                if e + 1 < NX:
                    xgT_copy(e + 1, (e + 1) % 2)
                y_out(e - 2, e % 2, (e + 2) % 4)


def kernel(x, L0_tok_A, L0_tok_B, L0_attn_Wq, L0_attn_bq, L0_attn_Wk, L0_attn_bk, L0_attn_Wv, L0_attn_bv,
           L0_attn_Wo, L0_attn_bo, L0_ffn_Wr, L0_ffn_W1, L0_ffn_b1, L0_ffn_W2, L0_ffn_b2):
    import numpy as np
    import concourse.bacc as bacc
    from concourse.bass_utils import run_bass_kernel_spmd

    P_ = 128
    c = np.ascontiguousarray
    x, A, B = np.asarray(x), np.asarray(L0_tok_A), np.asarray(L0_tok_B)
    E = B.shape[1]
    W1, W2 = np.asarray(L0_ffn_W1), np.asarray(L0_ffn_W2)
    NX, SUB, _, MID = W1.shape
    K = W2.shape[3]
    arrays = {
        "ids": c(x.reshape(-1, 64, 4, 2).transpose(3, 1, 0, 2)).reshape(P_, -1),
        "A": c(A), "B": c(B),
        "WqT": c(np.asarray(L0_attn_Wq).T), "WkT": c(np.asarray(L0_attn_Wk).T),
        "WvT": c(np.asarray(L0_attn_Wv).T), "WoT": c(np.asarray(L0_attn_Wo).T),
        "bqkv": c(np.concatenate([np.asarray(v).reshape(-1, P_) for v in (L0_attn_bq, L0_attn_bk, L0_attn_bv)]).T),
        "bo": c(np.asarray(L0_attn_bo).reshape(1, E)),
        "WrT": c(np.asarray(L0_ffn_Wr).T),
        "W1": c(W1.reshape(NX, SUB, E // P_, P_, MID).transpose(0, 3, 2, 1, 4)).reshape(NX, P_, -1),
        "b1T": c(np.asarray(L0_ffn_b1).reshape(-1, P_).T),
        "W2": c(W2.reshape(NX, SUB, MID // P_, P_, K).transpose(0, 3, 1, 2, 4)).reshape(NX, P_, -1),
        "b2T": c(np.asarray(L0_ffn_b2).reshape(-1, P_).T),
    }
    nc = bacc.Bacc("TRN2", target_bir_lowering=False, num_devices=1)
    args = [nc.dram_tensor(n, a.shape, mybir.dt.from_np(a.dtype), kind="ExternalInput").ap() for n, a in arrays.items()]
    args.append(nc.dram_tensor("out", (x.size, E), F32, kind="ExternalOutput").ap())
    tower_kernel(nc, *args)
    r = run_bass_kernel_spmd(nc, [arrays], core_ids=[0])
    return r.results[0]["out"].reshape(*x.shape, E)
```
